# Optimizing a Trainium2 kernel written in Bass

```python
import numpy as np
import jax
import jax.numpy as jnp

def _softmax(x, axis=-1):
    return jax.nn.softmax(x, axis=axis)

def _gelu(x):
    return jax.nn.gelu(x, approximate=True)

def _silu(x):
    return jax.nn.silu(x)

def _sigmoid(x):
    return jax.nn.sigmoid(x)

def _layernorm(x, axis=-1, eps=1e-05):
    m = jnp.mean(x, axis=axis, keepdims=True)
    v = jnp.var(x, axis=axis, keepdims=True)
    return (x - m) / jnp.sqrt(v + eps)

def _scatter_add(tgt, idx, src, axis=0):
    return tgt.at[idx].add(src)

def _segment_sum(src, seg, n):
    return jax.ops.segment_sum(src, seg, n)
kernel_name = 'mk_flamingo_gated_d1_seqx_r4_caf075'

def setup_inputs(seed: int=0):
    np.random.seed(seed)
    _w = jnp.asarray

    def _rec_inputs():
        import jax
        import jax.numpy as jnp
        _rk = jax.random.key(seed)
        x = -0.0003929 + 0.9999 * jax.random.normal(jax.random.fold_in(_rk, 1), (32, 256, 256), jnp.float32)
        _lenS = 256 - jax.random.randint(jax.random.fold_in(_rk, 7), (32,), 0, max(1, 256 // 4) + 1, jnp.int32)
        _lenS2 = 77 - jax.random.randint(jax.random.fold_in(_rk, 8), (32,), 0, max(1, 77 // 4) + 1, jnp.int32)
        _ctx_768P = jax.random.normal(jax.random.fold_in(_rk, 11), (32, 16, 192), jnp.float32)
        _ctx_768c = jax.random.dirichlet(jax.random.fold_in(_rk, 511), 0.3 * jnp.ones((16,), jnp.float32), (32, 77))
        _ctx_768t = jnp.einsum('bsk,bkd->bsd', _ctx_768c, _ctx_768P)
        _ctx_768t = _ctx_768t * jax.lax.rsqrt(jnp.mean(jnp.square(_ctx_768t)) + 1e-12) * 0.953939
        ctx_768 = -0.00055796 + 0.999787 * (_ctx_768t + 0.3 * jax.random.normal(jax.random.fold_in(_rk, 611), (32, 77, 192), jnp.float32))
        _g = jax.random.normal(jax.random.fold_in(_rk, 9001), (2, 1), jnp.float32)
        _g = jnp.sign(_g) * jnp.maximum(jnp.abs(_g), 1.0) + (_g == 0) * 1.0
        g_xattn = _g[0]
        g_ffn = _g[1]
        return (x, ctx_768, g_xattn, g_ffn)
    x, ctx_768, g_xattn, g_ffn = _rec_inputs()

    def _L0_xattn_setup():
        import jax, jax.numpy as jnp
        import numpy as np
        IMAGE_DIM = 256
        TEXT_DIM = 192
        NUM_HEADS = 16
        HEAD_DIM = IMAGE_DIM // NUM_HEADS
        key = jax.random.key(seed)
        ks = jax.random.split(key, 14)
        B, N, M = (4, 1024, 128)
        s_img = 1.0 / np.sqrt(IMAGE_DIM)
        s_txt = 1.0 / np.sqrt(TEXT_DIM)
        s_ff = 1.0 / np.sqrt(2 * IMAGE_DIM)
        return {'x': jax.random.normal(ks[0], (B, N, IMAGE_DIM), jnp.float32), 'y': jax.random.normal(ks[1], (B, M, TEXT_DIM), jnp.float32), 'Wq': jax.random.normal(ks[2], (IMAGE_DIM, IMAGE_DIM), jnp.float32) * s_img, 'bq': jax.random.normal(ks[3], (IMAGE_DIM,), jnp.float32) * s_img, 'Wk': jax.random.normal(ks[4], (TEXT_DIM, IMAGE_DIM), jnp.float32) * s_txt, 'bk': jax.random.normal(ks[5], (IMAGE_DIM,), jnp.float32) * s_txt, 'Wv': jax.random.normal(ks[6], (TEXT_DIM, IMAGE_DIM), jnp.float32) * s_txt, 'bv': jax.random.normal(ks[7], (IMAGE_DIM,), jnp.float32) * s_txt, 'W1': jax.random.normal(ks[8], (IMAGE_DIM, 2 * IMAGE_DIM), jnp.float32) * s_img, 'b1': jax.random.normal(ks[9], (2 * IMAGE_DIM,), jnp.float32) * s_img, 'W2': jax.random.normal(ks[10], (2 * IMAGE_DIM, IMAGE_DIM), jnp.float32) * s_ff, 'b2': jax.random.normal(ks[11], (IMAGE_DIM,), jnp.float32) * s_ff}
    _L0_xattn_all = _L0_xattn_setup()
    _L0_xattn_in = {k: v for k, v in _L0_xattn_all.items() if k in ('Wq', 'bq', 'Wk', 'bk', 'Wv', 'bv', 'W1', 'b1', 'W2', 'b2')}
    del _L0_xattn_all

    def _L0_ffn_setup():
        import jax, jax.numpy as jnp
        import numpy as np
        B, S, D, E, K = (4, 512, 256, 8, 2)
        EPS, W_THRES, TEMP = (0.0001, 0.1, 1.0)
        key = jax.random.key(seed)
        k1, k2, k3, k4, k5 = jax.random.split(key, 5)
        x = jax.random.normal(k1, (B, S, D), dtype=jnp.float32)
        gate_W = jax.random.normal(k2, (D, E), dtype=jnp.float32) * 0.02
        gate_b = jnp.zeros((E,), dtype=jnp.float32)
        expert_W = jax.random.normal(k3, (E, D, D), dtype=jnp.float32) * 0.02
        expert_b = jnp.zeros((E, D), dtype=jnp.float32)
        return {'x': x, 'gate_W': gate_W, 'gate_b': gate_b, 'expert_W': expert_W, 'expert_b': expert_b}
    _L0_ffn_all = _L0_ffn_setup()
    _L0_ffn_in = {k: v for k, v in _L0_ffn_all.items() if k in ('gate_W', 'gate_b', 'expert_W', 'expert_b')}
    del _L0_ffn_all
    return {'x': x, 'ctx_768': ctx_768, 'g_xattn': g_xattn, 'g_ffn': g_ffn, 'L0_xattn_Wq': _L0_xattn_in['Wq'], 'L0_xattn_bq': _L0_xattn_in['bq'], 'L0_xattn_Wk': _L0_xattn_in['Wk'], 'L0_xattn_bk': _L0_xattn_in['bk'], 'L0_xattn_Wv': _L0_xattn_in['Wv'], 'L0_xattn_bv': _L0_xattn_in['bv'], 'L0_xattn_W1': _L0_xattn_in['W1'], 'L0_xattn_b1': _L0_xattn_in['b1'], 'L0_xattn_W2': _L0_xattn_in['W2'], 'L0_xattn_b2': _L0_xattn_in['b2'], 'L0_ffn_gate_W': _L0_ffn_in['gate_W'], 'L0_ffn_gate_b': _L0_ffn_in['gate_b'], 'L0_ffn_expert_W': _L0_ffn_in['expert_W'], 'L0_ffn_expert_b': _L0_ffn_in['expert_b']}

def reference(x, ctx_768, g_xattn, g_ffn, L0_xattn_Wq, L0_xattn_bq, L0_xattn_Wk, L0_xattn_bk, L0_xattn_Wv, L0_xattn_bv, L0_xattn_W1, L0_xattn_b1, L0_xattn_W2, L0_xattn_b2, L0_ffn_gate_W, L0_ffn_gate_b, L0_ffn_expert_W, L0_ffn_expert_b):
    import jax
    import jax.numpy as jnp

    def _L0_xattn_ref(x, y, Wq, bq, Wk, bk, Wv, bv, W1, b1, W2, b2):
        import jax, jax.numpy as jnp
        import numpy as np
        IMAGE_DIM = 256
        TEXT_DIM = 192
        NUM_HEADS = 16
        HEAD_DIM = IMAGE_DIM // NUM_HEADS
        B, N, _ = x.shape
        M = y.shape[1]
        q = (x @ Wq + bq).reshape(B, N, NUM_HEADS, HEAD_DIM)
        k = (y @ Wk + bk).reshape(B, M, NUM_HEADS, HEAD_DIM)
        v = (y @ Wv + bv).reshape(B, M, NUM_HEADS, HEAD_DIM)
        scale = 1.0 / np.sqrt(HEAD_DIM)
        scores = jnp.einsum('bnhd,bmhd->bhnm', q, k) * scale
        attn = jax.nn.softmax(scores, axis=-1)
        out = jnp.einsum('bhnm,bmhd->bnhd', attn, v).reshape(B, N, IMAGE_DIM)
        h = jax.nn.relu(out @ W1 + b1)
        return h @ W2 + b2

    def _L0_ffn_ref(x, gate_W, gate_b, expert_W, expert_b):
        import jax, jax.numpy as jnp
        import numpy as np
        B, S, D, E, K = (4, 512, 256, 8, 2)
        EPS, W_THRES, TEMP = (0.0001, 0.1, 1.0)
        scores = jnp.maximum((x @ gate_W + gate_b) / TEMP, EPS)
        p = jax.nn.softmax(scores, axis=-1)
        _, topk_idx = jax.lax.top_k(p, K)
        topk_mask = jax.nn.one_hot(topk_idx, E, dtype=p.dtype).sum(-2) > 0
        w = jnp.maximum(p, W_THRES)
        w_gather = jnp.take_along_axis(w, topk_idx, axis=-1)
        total = jax.lax.stop_gradient(w_gather.sum(-1, keepdims=True))
        w = w / total
        comb = jnp.where(topk_mask, w, jnp.zeros_like(w))
        y = jnp.einsum('bsd,edf->bsef', x, expert_W) + expert_b
        out = jnp.einsum('bsef,bse->bsf', y, comb) / K
        return out
    x = x + jnp.tanh(g_xattn[0]) * _L0_xattn_ref(_layernorm(x, axis=-1), ctx_768, L0_xattn_Wq, L0_xattn_bq, L0_xattn_Wk, L0_xattn_bk, L0_xattn_Wv, L0_xattn_bv, L0_xattn_W1, L0_xattn_b1, L0_xattn_W2, L0_xattn_b2)
    x = x + jnp.tanh(g_ffn[0]) * _L0_ffn_ref(_layernorm(x, axis=-1), L0_ffn_gate_W, L0_ffn_gate_b, L0_ffn_expert_W, L0_ffn_expert_b)
    return x

_drawn_inputs = setup_inputs


def setup_inputs(seed=0):
    import zlib

    import numpy as np

    out = dict(_drawn_inputs(seed))
    spreads = {'L0_ffn_gate_b': (0.0, 0.1), 'L0_ffn_expert_b': (0.0, 0.1)}
    factors = {'L0_xattn_bq': 5.745, 'L0_xattn_bk': 8.0}
    for name, (base, spread) in spreads.items():
        noise = np.random.default_rng([zlib.crc32(name.encode()), seed]).standard_normal(out[name].shape)
        drawn = base * np.exp(spread * noise) if base else spread * noise
        out[name] = jnp.asarray(drawn.astype(out[name].dtype))
    for name, factor in factors.items():
        out[name] = (out[name] * factor).astype(out[name].dtype)
    return out
```

```python
from contextlib import ExitStack

import concourse.bass as bass
from concourse import mybir

F32 = mybir.dt.float32
F32R = mybir.dt.float32r
F16 = mybir.dt.float16
ALU = mybir.AluOpType
ACT = mybir.ActivationFunctionType
AX = mybir.AxisListType

P = 128
B, N, D = 32, 256, 256
M, DT = 77, 192
MP = M + M % 2
H = 16
DH = D // H
HID = 2 * D
E = 8
T = N // P
KC = D // P
HC = HID // P
YC = 96
YK = DT // YC
SLOT = 64
SHIFT = 3 * DH
PAIRS = H // 2
DV = DH + 1
LN_EPS = 1e-5
EPS, W_THRES, TOP_K = 1e-4, 0.1, 2
SCALE = float(DH) ** -0.5
MAX_CHUNKS = [[(0, 6)], [(6, 2), (8, 4)], [(12, 4)]]
CONSTS = 7 + E + 8
GATE_OPS = 22
STEADY = 4
LAST = B - 2


def gated_block(nc, x, y, g_xattn, g_ffn, Wq, bq, Wk, bk, Wv, bv, W1, b1, W2, b2,
                gate_W, gate_b, expert_W, expert_b, out):
    x_pairs = x.rearrange("(i u) (p t) d -> i u p t d", u=2, t=T)
    y_pairs = y.rearrange("(i u) m d -> i u m d", u=2)
    out_pairs = out.rearrange("(i u) (p t) d -> i u p t d", u=2, t=T)

    with ExitStack() as ctx:
        def sb(name, shape, dt=F32):
            return ctx.enter_context(nc.sbuf_tensor(name, shape, dt))

        def bank(name):
            return ctx.enter_context(nc.psum_tensor(name, [P, 512], F32))

        def sem(name):
            return ctx.enter_context(nc.semaphore(name))

        wq_f = sb("wq_f", [P, KC, D])
        w1_f = sb("w1_f", [P, KC, HID])
        w2_f = sb("w2_f", [P, HC, D])
        we_f = sb("we_f", [P, KC, E * D])
        gw_f = sb("gw_f", [P, KC, E])
        wq_hi, wq_lo = sb("wq_hi", [P, KC, D], F32R), sb("wq_lo", [P, KC, D], F32R)
        w1_hi, w1_lo = sb("w1_hi", [P, KC, HID], F32R), sb("w1_lo", [P, KC, HID], F32R)
        w2_hi, w2_lo = sb("w2_hi", [P, HC, D], F32R), sb("w2_lo", [P, HC, D], F32R)
        we_hi, we_lo = sb("we_hi", [P, KC, E * D], F32R), sb("we_lo", [P, KC, E * D], F32R)
        gw_hi, gw_lo = sb("gw_hi", [P, KC, E], F32R), sb("gw_lo", [P, KC, E], F32R)
        wkv = sb("wkv", [YC, YK, 2 * D])
        eb = sb("eb", [E, D])
        bq_rows = sb("bq_rows", [P, D])
        bkv_rows = sb("bkv_rows", [M, 2 * D])
        b2_rows = sb("b2_rows", [P, D])
        b2g_rows = sb("b2g_rows", [P, D])
        gb_rows = sb("gb_rows", [P, E])
        b1_cols = sb("b1_cols", [P, HC])
        gates = sb("gates", [P, 2])
        tanh_g = sb("tanh_g", [P, 2])
        ffn_scale = sb("ffn_scale", [P, 1])
        ident32 = sb("ident32", [P, P])
        ident16 = sb("ident16", [P, P], F16)
        own_head = sb("own_head", [P, PAIRS, M], F16)
        rank = sb("rank", [P, T, E])
        minus_half, ln_eps = sb("minus_half", [P, T]), sb("ln_eps", [P, T])

        x_sb = sb("x_sb", [P, 2, T, D])
        y_sb = sb("y_sb", [M, 2, DT])
        xb = sb("xb", [P, 2, T, D])
        stats1, mv1 = sb("stats1", [P, T, 6]), sb("mv1", [P, T, 2])
        ve1, rstd1 = sb("ve1", [P, T]), sb("rstd1", [P, T])
        xn = sb("xn", [P, T, D])
        xnT_hi, xnT_lo = sb("xnT_hi", [P, KC, N], F32R), sb("xnT_lo", [P, KC, N], F32R)
        yT = sb("yT", [YC, YK, M])
        kv = sb("kv", [M, 2 * D])
        q = sb("q", [P, T, D])
        v_hi, v_lo = sb("v_hi", [M, 2, H, DV], F16), sb("v_lo", [M, 2, H, DV], F16)
        k_hi, q_hi = sb("k_hi", [M, D], F16), sb("q_hi", [P, T, D], F16)
        k_stack = sb("k_stack", [M, H, SLOT], F16)
        q_stack = sb("q_stack", [P, T, H, SLOT], F16)
        qhT = sb("qhT", [P, KC, N], F16)
        khT = sb("khT", [P, KC, M], F16)
        k_block = sb("k_block", [P, H, M], F16)
        row_max = sb("row_max", [P, T, H])
        kz = sb("kz", [P, PAIRS, 2, M], F16)
        qsT = sb("qsT", [P, PAIRS, N], F16)
        RING = 4
        p_f = sb("p_f", [M, RING, 2 * N])
        p_hi = sb("p_hi", [M, RING, 2, N], F16)
        p_lo = sb("p_lo", [M, RING, 2, N], F16)
        rden = sb("rden", [P, 2, T, H // 2])
        o = sb("o", [P, T, D])
        oT_hi, oT_lo = sb("oT_hi", [P, KC, N], F32R), sb("oT_lo", [P, KC, N], F32R)
        h_f = sb("h_f", [P, HC, N])
        h_hi, h_lo = sb("h_hi", [P, HC, N], F32R), sb("h_lo", [P, HC, N], F32R)
        x1 = sb("x1", [P, 2, T, D])
        stats2, mv2 = sb("stats2", [P, T, 6]), sb("mv2", [P, T, 2])
        ve2, rstd2 = sb("ve2", [P, T]), sb("rstd2", [P, T])
        xn2 = sb("xn2", [P, T, D])
        x2T_hi, x2T_lo = sb("x2T_hi", [P, 2, KC, N], F32R), sb("x2T_lo", [P, 2, KC, N], F32R)
        gs, gshift, gexp, geq, gnot, gs2, gsel2, gmask, gp, gw = (
            sb(n, [P, T, E]) for n in ("gs", "gshift", "gexp", "geq", "gnot", "gs2", "gsel2", "gmask", "gp", "gw"))
        gm1, gf1, gm2, gf2, gsum, grs, gtot, grt = (
            sb(n, [P, T]) for n in ("gm1", "gf1", "gm2", "gf2", "gsum", "grs", "gtot", "grt"))
        comb = sb("comb", [P, 2, T, E])
        combT = sb("combT", [E, N])
        acc = sb("acc", [P, 2, T, D])

        G = [bank("g0"), bank("g1")]
        S = [bank("s0"), bank("s1")]
        TT = [bank("t0"), bank("t1")]
        X = [bank("e0"), bank("e1")]

        w_loaded = sem("w_loaded")
        consts_ready, waits_met = sem("consts_ready"), sem("waits_met")
        w_hi_ready, w_lo_ready = sem("w_hi_ready"), sem("w_lo_ready")
        tanh_ready, b2g_ready = sem("tanh_ready"), sem("b2g_ready")
        x_loaded = [sem("x_loaded0"), sem("x_loaded1")]
        y_loaded = [sem("y_loaded0"), sem("y_loaded1")]
        stats1_done, mv1_done = sem("stats1_done"), sem("mv1_done")
        ve1_done, rstd1_done, xn_done = sem("ve1_done"), sem("rstd1_done"), sem("xn_done")
        xb_done = sem("xb_done")
        xT_in_psum, yT_in_psum = sem("xT_in_psum"), sem("yT_in_psum")
        xnT_hi_done, xnT_lo_done, yT_done = sem("xnT_hi_done"), sem("xnT_lo_done"), sem("yT_done")
        kv_in_psum, q_in_psum = sem("kv_in_psum"), sem("q_in_psum")
        kv_done, q_done = sem("kv_done"), sem("q_done")
        v_split, k_split = sem("v_split"), sem("k_split")
        q_hi_done, q_lo_done, q_stacked = sem("q_hi_done"), sem("q_lo_done"), sem("q_stacked")
        hiT_in_psum, qhT_done, khT_done = sem("hiT_in_psum"), sem("qhT_done"), sem("khT_done")
        k_block_done = sem("k_block_done")
        max_scores, max_taken = sem("max_scores"), sem("max_taken")
        max_hi_done, max_lo_done = sem("max_hi_done"), sem("max_lo_done")
        kz_in_psum, kz_done = sem("kz_in_psum"), sem("kz_done")
        qs_in_psum = sem("qs_in_psum")
        qsa_done, qsb_done = sem("qsa_done"), sem("qsb_done")
        scores_ready, exps_done = sem("scores_ready"), sem("exps_done")
        p_lo_vector, p_lo_pool = sem("p_lo_vector"), sem("p_lo_pool")
        av_done = sem("av_done")
        rden_done, o_done = sem("rden_done"), sem("o_done")
        oT_in_psum, oT_hi_done, oT_lo_done = sem("oT_in_psum"), sem("oT_hi_done"), sem("oT_lo_done")
        h_in_psum, relu_done = sem("h_in_psum"), sem("relu_done")
        h_hi_done, h_lo_done = sem("h_hi_done"), sem("h_lo_done")
        mlp_in_psum, x1_done = sem("mlp_in_psum"), sem("x1_done")
        stats2_done, mv2_done = sem("stats2_done"), sem("mv2_done")
        ve2_done, rstd2_done, xn2_done = sem("ve2_done"), sem("rstd2_done"), sem("xn2_done")
        x2T_in_psum, x2T_hi_done, x2T_lo_done = sem("x2T_in_psum"), sem("x2T_hi_done"), sem("x2T_lo_done")
        gate_in_psum, gate_op, gate_exp = sem("gate_in_psum"), sem("gate_op"), sem("gate_exp")
        combT_in_psum, combT_done = sem("combT_in_psum"), sem("combT_done")
        bias_in_psum, acc_started = sem("bias_in_psum"), sem("acc_started")
        expert_in_psum, expert_added = sem("expert_in_psum"), sem("expert_added")
        stored = [sem("stored0"), sem("stored1")]

        block = ctx.enter_context(nc.Block())
        WEIGHTS = 17

        def at_least(eng, semaphore, value):
            if not isinstance(value, int) or value > 0:
                eng.wait_ge(semaphore, value)

        def apart(eng):
            eng.sem_inc(waits_met, 1)

        def row(pair, u, d):
            return pair + (u + d) // 2, (u + d) % 2, 2 * pair + u + d

        def run(eng, step, ahead=1):
            for s in range(STEADY):
                step(s // 2, s % 2, s)
            with eng.Fori(STEADY // 2, LAST // 2) as pair:
                for u in range(2):
                    step(pair, u, STEADY + u)
            for s in range(LAST, B + 2):
                step(s // 2, s % 2, s)

        def rows_to(count):
            return min(count, B) if isinstance(count, int) else count

        def has(s, d):
            return 0 <= s + d < B

        @block.sync
        def _(sp):
            for dst, src in [(wq_f[:], Wq.rearrange("(k p) n -> p k n", p=P)),
                             (wkv[:, :, 0:D], Wk.rearrange("(k p) n -> p k n", p=YC)),
                             (wkv[:, :, D:2 * D], Wv.rearrange("(k p) n -> p k n", p=YC)),
                             (bq_rows[:], bq.partition_broadcast(P)),
                             (bkv_rows[:, 0:D], bk.partition_broadcast(M)),
                             (bkv_rows[:, D:2 * D], bv.partition_broadcast(M)),
                             (gates[:, 0:1], g_xattn.partition_broadcast(P)),
                             (gates[:, 1:2], g_ffn.partition_broadcast(P)),
                             (b2_rows[:], b2.partition_broadcast(P)),
                             (gb_rows[:], gate_b.partition_broadcast(P)),
                             (eb[:], expert_b[:]),
                             (w1_f[:], W1.rearrange("(k p) n -> p k n", p=P)),
                             (w2_f[:], W2.rearrange("(k p) n -> p k n", p=P)),
                             (gw_f[:], gate_W.rearrange("(k p) n -> p k n", p=P))]:
                sp.dma_start(dst, src).then_inc(w_loaded, 16)
            sp.dma_start(b1_cols[:], b1.rearrange("(c p) -> p c", p=P), allow_slow_non_contiguous=True).then_inc(w_loaded, 16)
            for k in range(KC):
                sp.dma_start(we_f[:, k, :].rearrange("p (e f) -> p e f", e=E),
                             expert_W[:, k * P:(k + 1) * P, :].rearrange("e p f -> p e f")).then_inc(w_loaded, 16)
            for u in range(2):
                sp.wait_ge(stored[u], 16 * (B // 2))

        @block.gpsimd
        def _(pool):
            pool.memset(ident32[:], 0.0).then_inc(consts_ready, 1)
            pool.memset(ident16[:], 0.0).then_inc(consts_ready, 1)
            pool.memset(own_head[:], 1.0).then_inc(consts_ready, 1)
            pool.wait_ge(consts_ready, 3)
            for m in (ident32, ident16):
                pool.affine_select(out=m[:], in_=m[:], compare_op=ALU.not_equal, fill=1.0, base=0,
                                   pattern=[[-1, P]], channel_multiplier=1).then_inc(consts_ready, 1)
            pool.affine_select(out=own_head[:], in_=own_head[:], compare_op=ALU.is_ge, fill=0.0, base=0,
                               pattern=[[-DH, PAIRS], [0, M]], channel_multiplier=1).then_inc(consts_ready, 1)
            pool.wait_ge(consts_ready, 6)
            pool.affine_select(out=own_head[:], in_=own_head[:], compare_op=ALU.is_ge, fill=0.0, base=DH - 1,
                               pattern=[[DH, PAIRS], [0, M]], channel_multiplier=-1).then_inc(consts_ready, 1)
            for e in range(E):
                pool.memset(rank[:, :, e:e + 1], float(E - e)).then_inc(consts_ready, 1)
            pool.memset(minus_half[:], -0.5).then_inc(consts_ready, 1)
            pool.memset(ln_eps[:], LN_EPS).then_inc(consts_ready, 1)
            pool.memset(k_stack[:, :, SHIFT:SHIFT + 2], -1.0).then_inc(consts_ready, 1)
            pool.memset(k_stack[:, :, SHIFT + 2:SLOT], 0.0).then_inc(consts_ready, 1)
            pool.memset(q_stack[:, :, :, SHIFT + 2:SLOT], 0.0).then_inc(consts_ready, 1)
            pool.memset(kz[:], 0.0).then_inc(consts_ready, 1)
            pool.memset(v_hi[:, :, :, DH:DV], 1.0).then_inc(consts_ready, 1)
            pool.memset(v_lo[:, :, :, DH:DV], 0.0).then_inc(consts_ready, 1)
            pool.wait_ge(consts_ready, CONSTS)

            def first_norm_scale(b):
                pool.wait_ge(mv1_done, 2 * b + 2)
                pool.tensor_tensor(ve1[:], mv1[:, :, 1], ln_eps[:], ALU.add).then_inc(ve1_done, 1)
                pool.wait_ge(ve1_done, b + 1)
                at_least(pool, xn_done, 2 * b)
                pool.tensor_tensor(rstd1[:], ve1[:], minus_half[:], ALU.pow).then_inc(rstd1_done, 1)

            def second_norm_scale(b):
                pool.wait_ge(mv2_done, 2 * b + 2)
                pool.tensor_tensor(ve2[:], mv2[:, :, 1], ln_eps[:], ALU.add).then_inc(ve2_done, 1)
                pool.wait_ge(ve2_done, b + 1)
                pool.tensor_tensor(rstd2[:], ve2[:], minus_half[:], ALU.pow).then_inc(rstd2_done, 1)

            def x_with_bias(b, u):
                at_least(pool, x1_done, b - 1)
                pool.tensor_tensor(xb[:, u], x_sb[:, u], b2g_rows[:].unsqueeze(1).to_broadcast([P, T, D]),
                                   ALU.add).then_inc(xb_done, 1)

            def p_low(b, g):
                r = g % RING
                pool.wait_ge(exps_done, 16 * b + 2 * g + 2)
                pool.tensor_tensor(p_lo[:, r].rearrange("m h n -> m (h n)"), p_f[:, r, :],
                                   p_hi[:, r].rearrange("m h n -> m (h n)"), ALU.subtract).then_inc(p_lo_pool, 1)

            def k_high(b):
                pool.wait_ge(kv_done, b + 1)
                at_least(pool, hiT_in_psum, b)
                apart(pool)
                pool.tensor_copy(k_hi[:], kv[:, 0:D]).then_inc(k_split, 1)

            def k_rest(b):
                pool.wait_ge(k_split, 4 * b + 1)
                at_least(pool, kz_in_psum, b)
                high = k_hi[:].rearrange("m (h d) -> m h d", h=H)
                pool.tensor_tensor(k_stack[:, :, DH:2 * DH], kv[:, 0:D].rearrange("m (h d) -> m h d", h=H),
                                   high, ALU.subtract).then_inc(k_split, 1)
                pool.tensor_copy(k_stack[:, :, 0:DH], high).then_inc(k_split, 1)
                pool.tensor_copy(k_stack[:, :, 2 * DH:3 * DH], high).then_inc(k_split, 1)

            def q_low(b):
                pool.wait_ge(q_hi_done, b + 1)
                at_least(pool, qs_in_psum, 2 * b)
                pool.tensor_tensor(q_stack[:, :, :, 2 * DH:3 * DH].rearrange("p t h d -> p (t h) d"),
                                   q[:].rearrange("p t (h d) -> p (t h) d", h=H),
                                   q_hi[:].rearrange("p t (h d) -> p (t h) d", h=H),
                                   ALU.subtract).then_inc(q_lo_done, 1)

            def v_parts(b, u):
                at_least(pool, av_done, 8 * (b - 1))
                v = kv[:, D:2 * D].rearrange("m (h d) -> m h d", h=H)
                apart(pool)
                pool.tensor_copy(v_hi[:, u, :, 0:DH], v).then_inc(v_split, 1)
                pool.wait_ge(v_split, 2 * b + 1)
                pool.tensor_tensor(v_lo[:, u, :, 0:DH], v, v_hi[:, u, :, 0:DH], ALU.subtract).then_inc(v_split, 1)

            def key_blocks(b):
                pool.wait_ge(khT_done, b + 1)
                at_least(pool, max_scores, 6 * b)
                for c in range(KC):
                    pool.tensor_tensor(k_block[:, c * PAIRS:(c + 1) * PAIRS, :], own_head[:],
                                       khT[:, c, :].unsqueeze(1).to_broadcast([P, PAIRS, M]),
                                       ALU.mult).then_inc(k_block_done, 1)

            def h_high(b, c):
                pool.wait_ge(relu_done, 4 * b + 2 * c + 2)
                if c == 0:
                    at_least(pool, mlp_in_psum, b)
                apart(pool)
                pool.tensor_copy(h_hi[:, 2 * c:2 * c + 2, :], h_f[:, 2 * c:2 * c + 2, :]).then_inc(h_hi_done, 1)

            pool.wait_ge(b2g_ready, 1)
            pool.wait_ge(x_loaded[0], 16)
            first_norm_scale(0)
            x_with_bias(0, 0)

            def step(pair, u, s):
                _, _, b = row(pair, u, 0)
                _, mu, m = row(pair, u, -1)
                n_pair, nu, n = row(pair, u, 1)
                if has(s, -1):
                    p_low(m, 1)
                if has(s, 0):
                    k_high(b)
                if has(s, -1):
                    p_low(m, 3)
                    p_low(m, 5)
                if has(s, 0):
                    q_low(b)
                if has(s, -1):
                    p_low(m, 7)
                if has(s, 0):
                    key_blocks(b)
                if has(s, -1):
                    h_high(m, 0)
                    h_high(m, 1)
                if has(s, 0):
                    k_rest(b)
                    v_parts(b, u)
                if has(s, -1):
                    second_norm_scale(m)
                if has(s, 1):
                    first_norm_scale(n)
                    x_with_bias(n, nu)

            run(pool, step)

        @block.scalar
        def _(act):
            def load(pair, u, b):
                at_least(act, xn_done, 2 * (b - 1))
                at_least(act, xb_done, b - 1)
                act.dma_start(x_sb[:, u], x_pairs[pair, u]).then_inc(x_loaded[u], 16)
                at_least(act, yT_in_psum, b - 1)
                act.dma_start(y_sb[:, u], y_pairs[pair, u]).then_inc(y_loaded[u], 16)

            load(0, 0, 0)
            load(0, 1, 1)
            act.wait_ge(w_loaded, 16 * WEIGHTS)
            act.activation(tanh_g[:], gates[:], ACT.Tanh).then_inc(tanh_ready, 1)
            for hi, full in ((wq_hi, wq_f), (w1_hi, w1_f), (w2_hi, w2_f), (gw_hi, gw_f), (we_hi, we_f)):
                act.activation(hi[:], full[:], ACT.Copy).then_inc(w_hi_ready, 1)

            def xnT_high(b):
                act.wait_ge(xT_in_psum, b + 1)
                at_least(act, q_in_psum, b)
                act.activation(xnT_hi[:].rearrange("p k n -> p (k n)"), G[0][:], ACT.Copy).then_inc(xnT_hi_done, 1)

            def yT_copy(b):
                act.wait_ge(yT_in_psum, b + 1)
                at_least(act, kv_in_psum, b)
                act.activation(yT[:].rearrange("p k m -> p (k m)"), G[1][0:YC, 0:YK * M], ACT.Copy).then_inc(yT_done, 1)

            def combT_copy(b):
                act.wait_ge(combT_in_psum, b + 1)
                at_least(act, bias_in_psum, b)
                act.activation(combT[:], G[0][0:E, 0:N], ACT.Copy).then_inc(combT_done, 1)

            def exps(b, g):
                r = g % RING
                act.wait_ge(scores_ready, 8 * b + g + 1)
                at_least(act, av_done, 8 * b + g - RING + 1)
                act.activation(p_f[:, r, :], TT[g % 2][0:M, :], ACT.Exp, scale=SCALE).then_inc(exps_done, 1)
                act.activation(p_hi[:, r].rearrange("m h n -> m (h n)"), TT[g % 2][0:M, :], ACT.Exp,
                               scale=SCALE).then_inc(exps_done, 1)

            def q_stack_high(b):
                act.wait_ge(q_hi_done, b + 1)
                at_least(act, qs_in_psum, 2 * b)
                act.activation(q_stack[:, :, :, 0:2 * DH].rearrange("p t h (c d) -> p (t h) c d", c=2),
                               q_hi[:].rearrange("p t (h d) -> p (t h) d", h=H).unsqueeze(2).to_broadcast([P, T * H, 2, DH]),
                               ACT.Copy).then_inc(q_stacked, 1)

            def highT_copies(b):
                act.wait_ge(hiT_in_psum, b + 1)
                at_least(act, k_block_done, 2 * b)
                at_least(act, max_scores, 6 * b)
                src = G[0][:].bitcast(F16)
                act.activation(khT[:], src[:, KC * N:KC * (N + MP)].rearrange("p (k m) -> p k m", k=KC)[:, :, 0:M],
                               ACT.Copy).then_inc(khT_done, 1)
                act.activation(qhT[:].rearrange("p k n -> p (k n)"), src[:, 0:KC * N], ACT.Copy).then_inc(qhT_done, 1)

            def oT_high(b):
                act.wait_ge(oT_in_psum, b + 1)
                at_least(act, h_in_psum, 2 * b)
                act.activation(oT_hi[:].rearrange("p k n -> p (k n)"), G[1][:], ACT.Copy).then_inc(oT_hi_done, 1)

            def relus(b, c):
                act.wait_ge(h_in_psum, 2 * b + c + 1)
                at_least(act, h_lo_done, 2 * b)
                for j in range(2):
                    act.activation(h_f[:, 2 * c + j, :], G[c][:, j * N:(j + 1) * N], ACT.Relu,
                                   bias=b1_cols[:, 2 * c + j:2 * c + j + 1]).then_inc(relu_done, 1)

            def kz_copies(b):
                act.wait_ge(kz_in_psum, b + 1)
                at_least(act, scores_ready, 8 * b)
                src = G[1][:].bitcast(F16)[:, 0:PAIRS * MP].rearrange("p (j m) -> p j m", j=PAIRS)[:, :, 0:M]
                for e in range(2):
                    act.activation(kz[e * SLOT:(e + 1) * SLOT, :, e, :], src[e * SLOT:(e + 1) * SLOT],
                                   ACT.Copy).then_inc(kz_done, 1)

            def qs_copy_a(b):
                act.wait_ge(qs_in_psum, 2 * b + 1)
                act.activation(qsT[:, 0:4, :].rearrange("p j n -> p (j n)"), G[0][:].bitcast(F16), ACT.Copy).then_inc(qsa_done, 1)

            def x2T_high(b, u):
                act.wait_ge(x2T_in_psum, b + 1)
                at_least(act, expert_in_psum, 8 * (b - 1))
                at_least(act, gate_in_psum, b - 1)
                act.activation(x2T_hi[:, u].rearrange("p k n -> p (k n)"), G[0][:], ACT.Copy).then_inc(x2T_hi_done, 1)

            def gate_exps(b):
                act.wait_ge(gate_op, GATE_OPS * b + 4)
                act.activation(gexp[:], gshift[:], ACT.Exp).then_inc(gate_exp, 1)

            def store(pair, u, b):
                act.wait_ge(expert_added, 16 * b + 16)
                act.dma_start(out_pairs[pair, u], acc[:, u]).then_inc(stored[u], 16)

            def step(pair, u, s):
                _, _, b = row(pair, u, 0)
                _, mu, m = row(pair, u, -1)
                e_pair, eu, e = row(pair, u, -2)
                l_pair, lu, l = row(pair, u, 2)
                if has(s, 0):
                    xnT_high(b)
                    yT_copy(b)
                if has(s, -1):
                    exps(m, 0)
                    exps(m, 1)
                if has(s, -2):
                    combT_copy(e)
                if has(s, -1):
                    exps(m, 2)
                    exps(m, 3)
                    exps(m, 4)
                if has(s, 0):
                    q_stack_high(b)
                if has(s, -1):
                    exps(m, 5)
                    exps(m, 6)
                if has(s, 0):
                    highT_copies(b)
                if has(s, -1):
                    exps(m, 7)
                    oT_high(m)
                    relus(m, 0)
                    relus(m, 1)
                if has(s, 0):
                    kz_copies(b)
                    qs_copy_a(b)
                if has(s, 2):
                    load(l_pair, lu, l)
                if has(s, -1):
                    x2T_high(m, mu)
                    gate_exps(m)
                if has(s, -2):
                    store(e_pair, eu, e)

            run(act, step)

        @block.tensor
        def _(pe):
            pe.wait_ge(consts_ready, CONSTS)
            pe.wait_ge(w_loaded, 16 * WEIGHTS)
            pe.wait_ge(w_hi_ready, 5)
            pe.wait_ge(w_lo_ready, 5)

            def split_product(out_ap, pairs):
                n = 3 * len(pairs)
                i = 0
                for s_hi, s_lo, m_hi, m_lo in pairs:
                    for a, c in ((s_lo, m_hi), (s_hi, m_lo), (s_hi, m_hi)):
                        mm = pe.matmul(out_ap, a, c, start=(i == 0), stop=(i == n - 1))
                        i += 1
                return mm

            def transposes_xy(b, u):
                pe.wait_ge(xn_done, 2 * b + 2)
                at_least(pe, x2T_lo_done, b - 1)
                at_least(pe, qsa_done, b)
                for k in range(KC):
                    for t in range(T):
                        mm = pe.transpose(G[0][:, k * N + t * P:k * N + (t + 1) * P], xn[:, t, k * P:(k + 1) * P], ident32[:])
                mm.then_inc(xT_in_psum, 1)

            def transposes_y(pair, b, u):
                pe.wait_ge(y_loaded[u], 16 * (pair + 1))
                at_least(pe, gate_op, GATE_OPS * (b - 2) + 1)
                at_least(pe, qsb_done, b)
                for k in range(YK):
                    mm = pe.transpose(G[1][0:YC, k * M:(k + 1) * M], y_sb[:, u, k * YC:(k + 1) * YC], ident32[0:M, 0:M])
                mm.then_inc(yT_in_psum, 1)

            def scores(b, g):
                if g == 0:
                    pe.wait_ge(kz_done, 2 * b + 2)
                    pe.wait_ge(qsa_done, b + 1)
                    pe.wait_ge(qsb_done, b + 1)
                at_least(pe, exps_done, 2 * (8 * b + g - 1))
                for e in range(2):
                    mm = pe.matmul(TT[g % 2][0:M, e * N:(e + 1) * N], kz[:, g, e, :], qsT[:, g, :],
                                   start=True, stop=True)
                mm.then_inc(scores_ready, 1)

            def attend(b, u, g):
                if g == 0:
                    pe.wait_ge(v_split, 2 * b + 2)
                    pe.wait_ge(max_taken, 6 * b + 6)
                if g % 2 == 0:
                    pe.wait_ge(p_lo_vector, 4 * b + g // 2 + 1)
                else:
                    pe.wait_ge(p_lo_pool, 4 * b + g // 2 + 1)
                r, half = g % RING, g // 4
                for e in range(2):
                    h = 2 * g + e
                    for t in range(T):
                        at = (t * (H // 2) + h % (H // 2)) * DV
                        hi, lo = p_hi[:, r, e, t * P:(t + 1) * P], p_lo[:, r, e, t * P:(t + 1) * P]
                        dst = S[half][:, at:at + DV]
                        pe.matmul(dst, lo, v_hi[:, u, h, :], start=True, stop=False)
                        pe.matmul(dst, hi, v_lo[:, u, h, :], start=False, stop=False)
                        mm = pe.matmul(dst, hi, v_hi[:, u, h, :], start=False, stop=True)
                mm.then_inc(av_done, 1)

            def combT_transposes(b, u):
                pe.wait_ge(gate_op, GATE_OPS * b + GATE_OPS)
                pe.wait_ge(x2T_lo_done, b + 1)
                at_least(pe, xnT_lo_done, rows_to(b + 3))
                for t in range(T):
                    mm = pe.transpose(G[0][0:E, t * P:(t + 1) * P], comb[:, u, t, :], ident32[:])
                mm.then_inc(combT_in_psum, 1)

            def expert_biases(b):
                pe.wait_ge(combT_done, b + 1)
                at_least(pe, yT_done, rows_to(b + 3))
                for t in range(T):
                    mm = pe.matmul(G[1][:, t * D:(t + 1) * D], combT[:, t * P:(t + 1) * P], eb[:], start=True, stop=True)
                mm.then_inc(bias_in_psum, 1)

            def keys_values(b):
                pe.wait_ge(yT_done, b + 1)
                at_least(pe, combT_done, b - 1)
                pe.wait_ge(xnT_lo_done, b + 1)
                for k in range(YK):
                    mm = pe.matmul(G[0][0:M, :], yT[:, k, :], wkv[:, k, :], start=(k == 0), stop=(k == YK - 1))
                mm.then_inc(kv_in_psum, 1)

            def queries(b):
                pe.wait_ge(xnT_lo_done, b + 1)
                pe.wait_ge(yT_done, b + 1)
                at_least(pe, acc_started, b - 1)
                for t in range(T):
                    rows = slice(t * P, (t + 1) * P)
                    mm = split_product(G[1][:, t * D:(t + 1) * D],
                                       [(xnT_hi[:, k, rows], xnT_lo[:, k, rows], wq_hi[:, k, :], wq_lo[:, k, :])
                                        for k in range(KC)])
                mm.then_inc(q_in_psum, 1)

            def high_transposes(b):
                pe.wait_ge(q_hi_done, b + 1)
                pe.wait_ge(k_split, 4 * b + 1)
                pe.wait_ge(kv_done, b + 1)
                dst = G[0][:].bitcast(F16)
                for c in range(KC):
                    for t in range(T):
                        pe.transpose(dst[:, c * N + t * P:c * N + (t + 1) * P], q_hi[:, t, c * P:(c + 1) * P], ident16[:])
                    mm = pe.transpose(dst[:, KC * N + c * MP:KC * N + c * MP + M], k_hi[:, c * P:(c + 1) * P],
                                      ident16[0:M, 0:M])
                mm.then_inc(hiT_in_psum, 1)

            def scores_for_max(b, i):
                t, c = divmod(i, len(MAX_CHUNKS))
                if i == 0:
                    pe.wait_ge(qhT_done, b + 1)
                    pe.wait_ge(k_block_done, 2 * b + 2)
                if i < 2:
                    at_least(pe, o_done, 4 * b - 2 + 2 * i)
                else:
                    pe.wait_ge(max_taken, 6 * b + i - 1)
                at = 0
                for h, n in MAX_CHUNKS[c]:
                    mm = pe.matmul(S[i % 2][:, at * M:(at + n) * M], qhT[:, h // PAIRS, t * P:(t + 1) * P],
                                   k_block[:, h:h + n, :], start=True, stop=True)
                    at += n
                mm.then_inc(max_scores, 1)

            def output_transposes(b):
                pe.wait_ge(o_done, 4 * b + 4)
                at_least(pe, q_done, rows_to(b + 2))
                at_least(pe, acc_started, b)
                for k in range(KC):
                    for t in range(T):
                        mm = pe.transpose(G[1][:, k * N + t * P:k * N + (t + 1) * P], o[:, t, k * P:(k + 1) * P], ident32[:])
                mm.then_inc(oT_in_psum, 1)

            def mlp_up(b, c):
                pe.wait_ge(oT_lo_done, b + 1)
                if c == 0:
                    at_least(pe, combT_done, b)
                    at_least(pe, qhT_done, rows_to(b + 2))
                    at_least(pe, khT_done, rows_to(b + 2))
                for j in range(2):
                    cols = slice((2 * c + j) * P, (2 * c + j + 1) * P)
                    mm = split_product(G[c][:, j * N:(j + 1) * N],
                                       [(w1_hi[:, k, cols], w1_lo[:, k, cols], oT_hi[:, k, :], oT_lo[:, k, :])
                                        for k in range(KC)])
                mm.then_inc(h_in_psum, 1)

            def mlp_down(b):
                pe.wait_ge(h_lo_done, 2 * b + 2)
                pe.wait_ge(relu_done, 4 * b + 4)
                for t in range(T):
                    rows = slice(t * P, (t + 1) * P)
                    mm = split_product(G[0][:, t * D:(t + 1) * D],
                                       [(h_hi[:, c, rows], h_lo[:, c, rows], w2_hi[:, c, :], w2_lo[:, c, :])
                                        for c in range(HC)])
                mm.then_inc(mlp_in_psum, 1)

            def key_stack_transposes(b):
                pe.wait_ge(k_split, 4 * b + 4)
                at_least(pe, relu_done, 4 * b)
                pe.wait_ge(q_done, b + 1)
                dst = G[1][:].bitcast(F16)
                for j in range(PAIRS):
                    mm = pe.transpose(dst[:, j * MP:j * MP + M], k_stack[:, 2 * j:2 * j + 2, :].rearrange("m h r -> m (h r)"),
                                      ident16[0:M, 0:M])
                mm.then_inc(kz_in_psum, 1)

            def query_stack_transposes(b, c):
                if c == 0:
                    pe.wait_ge(q_lo_done, b + 1)
                    pe.wait_ge(q_stacked, b + 1)
                    pe.wait_ge(max_lo_done, b + 1)
                    at_least(pe, x1_done, b)
                    pe.wait_ge(qhT_done, b + 1)
                else:
                    pe.wait_ge(kz_done, 2 * b + 2)
                dst = G[c][:].bitcast(F16)
                for j in range(4):
                    for t in range(T):
                        mm = pe.transpose(dst[:, j * N + t * P:j * N + (t + 1) * P],
                                          q_stack[:, t, 8 * c + 2 * j:8 * c + 2 * j + 2, :].rearrange("p h r -> p (h r)"),
                                          ident16[:])
                mm.then_inc(qs_in_psum, 1)

            def second_norm_transposes(b):
                pe.wait_ge(xn2_done, 2 * b + 2)
                at_least(pe, qsa_done, rows_to(b + 2))
                for k in range(KC):
                    for t in range(T):
                        mm = pe.transpose(G[0][:, k * N + t * P:k * N + (t + 1) * P], xn2[:, t, k * P:(k + 1) * P], ident32[:])
                mm.then_inc(x2T_in_psum, 1)

            def gate_scores(b, u):
                pe.wait_ge(x2T_lo_done, b + 1)
                at_least(pe, qsb_done, rows_to(b + 2))
                for t in range(T):
                    rows = slice(t * P, (t + 1) * P)
                    mm = split_product(G[1][:, t * E:(t + 1) * E],
                                       [(x2T_hi[:, u, k, rows], x2T_lo[:, u, k, rows], gw_hi[:, k, :], gw_lo[:, k, :])
                                        for k in range(KC)])
                mm.then_inc(gate_in_psum, 1)

            def experts(b, u, i):
                t, c = i % T, i // T
                at_least(pe, expert_added, 16 * b + 2 * (i - 1))
                rows, cols = slice(t * P, (t + 1) * P), slice(c * 2 * D, (c + 1) * 2 * D)
                mm = split_product(X[i % 2][:],
                                   [(x2T_hi[:, u, k, rows], x2T_lo[:, u, k, rows], we_hi[:, k, cols], we_lo[:, k, cols])
                                    for k in range(KC)])
                mm.then_inc(expert_in_psum, 1)

            def step(pair, u, s):
                _, _, b = row(pair, u, 0)
                _, mu, m = row(pair, u, -1)
                _, eu, e = row(pair, u, -2)
                front, mid, last = has(s, 0), has(s, -1), has(s, -2)
                if front:
                    transposes_xy(b, u)
                    transposes_y(pair, b, u)
                if mid:
                    scores(m, 0)
                    scores(m, 1)
                if last:
                    combT_transposes(e, eu)
                if mid:
                    attend(m, mu, 0)
                    scores(m, 2)
                if last:
                    expert_biases(e)
                    experts(e, eu, 0)
                if mid:
                    attend(m, mu, 1)
                    scores(m, 3)
                if front:
                    keys_values(b)
                if mid:
                    attend(m, mu, 2)
                    scores(m, 4)
                if front:
                    queries(b)
                if mid:
                    attend(m, mu, 3)
                    scores(m, 5)
                if last:
                    experts(e, eu, 1)
                if mid:
                    attend(m, mu, 4)
                    scores(m, 6)
                if front:
                    high_transposes(b)
                if mid:
                    attend(m, mu, 5)
                    scores(m, 7)
                if last:
                    experts(e, eu, 2)
                if mid:
                    attend(m, mu, 6)
                    attend(m, mu, 7)
                if front:
                    scores_for_max(b, 0)
                if last:
                    experts(e, eu, 3)
                if mid:
                    output_transposes(m)
                if front:
                    scores_for_max(b, 1)
                    scores_for_max(b, 2)
                if mid:
                    mlp_up(m, 0)
                if front:
                    scores_for_max(b, 3)
                if mid:
                    mlp_up(m, 1)
                if front:
                    scores_for_max(b, 4)
                if last:
                    experts(e, eu, 4)
                if front:
                    scores_for_max(b, 5)
                if mid:
                    mlp_down(m)
                if last:
                    experts(e, eu, 5)
                if front:
                    key_stack_transposes(b)
                    query_stack_transposes(b, 0)
                    query_stack_transposes(b, 1)
                if last:
                    experts(e, eu, 6)
                if mid:
                    second_norm_transposes(m)
                if last:
                    experts(e, eu, 7)
                if mid:
                    gate_scores(m, mu)

            run(pe, step)

        @block.vector
        def _(dve):
            for i, (lo, hi, full) in enumerate(((wq_lo, wq_hi, wq_f), (w1_lo, w1_hi, w1_f), (w2_lo, w2_hi, w2_f),
                                                (gw_lo, gw_hi, gw_f), (we_lo, we_hi, we_f))):
                dve.wait_ge(w_hi_ready, i + 1)
                if i == 0:
                    dve.wait_ge(w_loaded, 16 * WEIGHTS)
                dve.tensor_tensor(lo[:], full[:], hi[:].bitcast(F32), ALU.subtract).then_inc(w_lo_ready, 1)
            dve.wait_ge(tanh_ready, 1)
            dve.tensor_scalar(b2g_rows[:], b2_rows[:], tanh_g[:, 0:1], None, ALU.mult).then_inc(b2g_ready, 1)
            dve.tensor_scalar(ffn_scale[:], tanh_g[:, 1:2], 1.0 / TOP_K, None, ALU.mult).then_inc(b2g_ready, 1)
            dve.wait_ge(b2g_ready, 2)
            dve.wait_ge(consts_ready, CONSTS)

            def first_norm_stats(pair, b, u):
                dve.wait_ge(x_loaded[u], 16 * (pair + 1))
                for t in range(T):
                    dve.bn_stats(stats1[:, t, :], x_sb[:, u, t, :]).then_inc(stats1_done, 1)
                for t in range(T):
                    dve.wait_ge(stats1_done, 2 * b + t + 1)
                    apart(dve)
                    dve.bn_aggr(mv1[:, t, :], stats1[:, t, :]).then_inc(mv1_done, 1)

            def first_norm(b, u):
                dve.wait_ge(rstd1_done, b + 1)
                dve.wait_ge(mv1_done, 2 * b + 2)
                at_least(dve, xT_in_psum, b)
                for t in range(T):
                    dve.tensor_scalar(xn[:, t, :], x_sb[:, u, t, :], mv1[:, t, 0:1], rstd1[:, t:t + 1],
                                      ALU.subtract, ALU.mult).then_inc(xn_done, 1)

            def xnT_low(b):
                dve.wait_ge(xnT_hi_done, b + 1)
                dve.tensor_tensor(xnT_lo[:].rearrange("p k n -> p (k n)"), G[0][:],
                                  xnT_hi[:].bitcast(F32).rearrange("p k n -> p (k n)"), ALU.subtract).then_inc(xnT_lo_done, 1)

            def p_low(b, g):
                r = g % RING
                dve.wait_ge(exps_done, 16 * b + 2 * g + 2)
                dve.tensor_tensor(p_lo[:, r].rearrange("m h n -> m (h n)"), p_f[:, r, :],
                                  p_hi[:, r].rearrange("m h n -> m (h n)"), ALU.subtract).then_inc(p_lo_vector, 1)

            def start_acc(pair, b, u):
                dve.wait_ge(bias_in_psum, b + 1)
                at_least(dve, stored[u], 16 * pair)
                dve.tensor_tensor(acc[:, u].rearrange("p t d -> p (t d)"), G[1][:],
                                  x1[:, u].rearrange("p t d -> p (t d)"), ALU.add).then_inc(acc_started, 1)

            def add_experts(b, u, i):
                t, c = i % T, i // T
                dve.wait_ge(expert_in_psum, 8 * b + i + 1)
                if i < 2:
                    dve.wait_ge(acc_started, b + 1)
                for j in range(2):
                    if j == 1:
                        dve.wait_ge(expert_added, 16 * b + 2 * i + 1)
                    elif i >= 2:
                        dve.wait_ge(expert_added, 16 * b + 2 * i - 2)
                    dve.scalar_tensor_tensor(out=acc[:, u, t, :], in0=X[i % 2][:, j * D:(j + 1) * D],
                                             scalar=comb[:, u, t, 2 * c + j:2 * c + j + 1], in1=acc[:, u, t, :],
                                             op0=ALU.mult, op1=ALU.add).then_inc(expert_added, 1)

            def kv_with_bias(b):
                dve.wait_ge(kv_in_psum, b + 1)
                at_least(dve, k_split, 4 * b)
                at_least(dve, v_split, 2 * b)
                dve.tensor_tensor(kv[:], G[0][0:M, :], bkv_rows[:], ALU.add).then_inc(kv_done, 1)

            def q_with_bias(b):
                dve.wait_ge(q_in_psum, b + 1)
                at_least(dve, q_lo_done, b)
                dve.tensor_tensor(q[:], G[1][:].rearrange("p (t d) -> p t d", t=T),
                                  bq_rows[:].unsqueeze(1).to_broadcast([P, T, D]), ALU.add).then_inc(q_done, 1)
                dve.wait_ge(q_done, b + 1)
                at_least(dve, hiT_in_psum, b)
                at_least(dve, q_stacked, b)
                dve.tensor_copy(q_hi[:], q[:]).then_inc(q_hi_done, 1)

            def normalise(b, half):
                dve.wait_ge(av_done, 8 * b + 4 * half + 4)
                src = S[half][:, 0:T * (H // 2) * DV].rearrange("p (t h d) -> p t h d", t=T, h=H // 2)
                dve.reciprocal(rden[:, half], src[:, :, :, DH]).then_inc(rden_done, 1)
                dve.wait_ge(rden_done, 2 * b + half + 1)
                if half == 0:
                    at_least(dve, oT_in_psum, b)
                for t in range(T):
                    dve.tensor_tensor(o[:, t, half * P:(half + 1) * P].rearrange("p (h d) -> p h d", h=H // 2),
                                      src[:, t, :, 0:DH],
                                      rden[:, half, t, :].unsqueeze(2).to_broadcast([P, H // 2, DH]),
                                      ALU.mult).then_inc(o_done, 1)

            def take_max(b, i):
                t, c = divmod(i, len(MAX_CHUNKS))
                h, n = MAX_CHUNKS[c][0][0], sum(k for _, k in MAX_CHUNKS[c])
                dve.wait_ge(max_scores, 6 * b + i + 1)
                if i == 0:
                    at_least(dve, max_lo_done, b)
                dve.tensor_reduce(row_max[:, t, h:h + n], S[i % 2][:, 0:n * M].rearrange("p (h m) -> p h m", h=n),
                                  AX.X, ALU.max).then_inc(max_taken, 1)

            def stack_max(b):
                dve.wait_ge(max_taken, 6 * b + 6)
                at_least(dve, qs_in_psum, 2 * b)
                flat = q_stack[:].rearrange("p t h r -> p (t h) r")
                mx = row_max[:].rearrange("p t h -> p (t h)")
                dve.tensor_copy(flat[:, :, SHIFT], mx).then_inc(max_hi_done, 1)
                dve.wait_ge(max_hi_done, b + 1)
                dve.tensor_tensor(flat[:, :, SHIFT + 1], mx, flat[:, :, SHIFT], ALU.subtract).then_inc(max_lo_done, 1)

            def oT_low(b):
                dve.wait_ge(oT_hi_done, b + 1)
                dve.tensor_tensor(oT_lo[:].rearrange("p k n -> p (k n)"), G[1][:],
                                  oT_hi[:].bitcast(F32).rearrange("p k n -> p (k n)"), ALU.subtract).then_inc(oT_lo_done, 1)

            def h_low(b, c):
                dve.wait_ge(h_hi_done, 2 * b + c + 1)
                part = slice(2 * c, 2 * c + 2)
                dve.tensor_tensor(h_lo[:, part, :], h_f[:, part, :], h_hi[:, part, :].bitcast(F32),
                                  ALU.subtract).then_inc(h_lo_done, 1)

            def add_mlp(b, u):
                dve.wait_ge(mlp_in_psum, b + 1)
                dve.wait_ge(xb_done, b + 1)
                dve.scalar_tensor_tensor(out=x1[:, u].rearrange("p t d -> p (t d)"), in0=G[0][:], scalar=tanh_g[:, 0:1],
                                         in1=xb[:, u].rearrange("p t d -> p (t d)"), op0=ALU.mult, op1=ALU.add)\
                   .then_inc(x1_done, 1)

            def second_norm_stats(b, u):
                dve.wait_ge(x1_done, b + 1)
                for t in range(T):
                    dve.bn_stats(stats2[:, t, :], x1[:, u, t, :]).then_inc(stats2_done, 1)
                for t in range(T):
                    dve.wait_ge(stats2_done, 2 * b + t + 1)
                    apart(dve)
                    dve.bn_aggr(mv2[:, t, :], stats2[:, t, :]).then_inc(mv2_done, 1)

            def second_norm(b, u):
                dve.wait_ge(rstd2_done, b + 1)
                for t in range(T):
                    dve.tensor_scalar(xn2[:, t, :], x1[:, u, t, :], mv2[:, t, 0:1], rstd2[:, t:t + 1],
                                      ALU.subtract, ALU.mult).then_inc(xn2_done, 1)

            def x2T_low(b, u):
                dve.wait_ge(x2T_hi_done, b + 1)
                dve.tensor_tensor(x2T_lo[:, u].rearrange("p k n -> p (k n)"), G[0][:],
                                  x2T_hi[:, u].bitcast(F32).rearrange("p k n -> p (k n)"), ALU.subtract).then_inc(x2T_lo_done, 1)

            def qs_copy_b(b):
                dve.wait_ge(qs_in_psum, 2 * b + 2)
                dve.tensor_copy(qsT[:, 4:8, :].rearrange("p j n -> p (j n)"), G[1][:].bitcast(F16)).then_inc(qsb_done, 1)

            def gating(b, u):
                done = [0]

                def link(ins):
                    done[0] += 1
                    ins.then_inc(gate_op, 1)
                    dve.wait_ge(gate_op, GATE_OPS * b + done[0])

                def wide(a):
                    return a[:].unsqueeze(2).to_broadcast([P, T, E])

                dve.wait_ge(gate_in_psum, b + 1)
                link(dve.tensor_tensor(gs[:], G[1][:, 0:T * E].rearrange("p (t e) -> p t e", t=T),
                                       gb_rows[:].unsqueeze(1).to_broadcast([P, T, E]), ALU.add))
                link(dve.tensor_scalar(gs[:], gs[:], EPS, None, ALU.max))
                link(dve.tensor_reduce(gm1[:], gs[:], AX.X, ALU.max))
                link(dve.tensor_tensor(gshift[:], gs[:], wide(gm1), ALU.subtract))
                link(dve.tensor_tensor(geq[:], gs[:], wide(gm1), ALU.is_equal))
                link(dve.tensor_tensor(geq[:], geq[:], rank[:], ALU.mult))
                link(dve.tensor_reduce(gf1[:], geq[:], AX.X, ALU.max))
                link(dve.tensor_tensor(gnot[:], rank[:], wide(gf1), ALU.not_equal))
                link(dve.tensor_tensor(gs2[:], gs[:], gnot[:], ALU.mult))
                link(dve.tensor_reduce(gm2[:], gs2[:], AX.X, ALU.max))
                link(dve.tensor_tensor(geq[:], gs2[:], wide(gm2), ALU.is_equal))
                link(dve.tensor_tensor(geq[:], geq[:], rank[:], ALU.mult))
                link(dve.tensor_reduce(gf2[:], geq[:], AX.X, ALU.max))
                link(dve.tensor_tensor(gsel2[:], rank[:], wide(gf2), ALU.is_equal))
                link(dve.scalar_tensor_tensor(out=gmask[:], in0=gsel2[:], scalar=1.0, in1=gnot[:],
                                              op0=ALU.add, op1=ALU.subtract))
                dve.wait_ge(gate_exp, b + 1)
                link(dve.tensor_reduce(gsum[:], gexp[:], AX.X, ALU.add))
                link(dve.reciprocal(grs[:], gsum[:]))
                link(dve.tensor_tensor(gp[:], gexp[:], wide(grs), ALU.mult))
                link(dve.scalar_tensor_tensor(out=gw[:], in0=gp[:], scalar=W_THRES, in1=gmask[:],
                                              op0=ALU.max, op1=ALU.mult))
                link(dve.tensor_reduce(gtot[:], gw[:], AX.X, ALU.add))
                link(dve.reciprocal(grt[:], gtot[:]))
                link(dve.scalar_tensor_tensor(out=comb[:, u], in0=gw[:], scalar=ffn_scale[:, 0:1], in1=wide(grt),
                                              op0=ALU.mult, op1=ALU.mult))
                assert done[0] == GATE_OPS

            def step(pair, u, s):
                _, _, b = row(pair, u, 0)
                _, mu, m = row(pair, u, -1)
                e_pair, eu, e = row(pair, u, -2)
                n_pair, nu, n = row(pair, u, 1)
                front, mid, last = has(s, 0), has(s, -1), has(s, -2)
                if front:
                    xnT_low(b)
                if mid:
                    p_low(m, 0)
                if last:
                    start_acc(e_pair, e, eu)
                    add_experts(e, eu, 0)
                if front:
                    kv_with_bias(b)
                if mid:
                    p_low(m, 2)
                if front:
                    q_with_bias(b)
                if mid:
                    p_low(m, 4)
                    normalise(m, 0)
                if last:
                    add_experts(e, eu, 1)
                if mid:
                    p_low(m, 6)
                if last:
                    add_experts(e, eu, 2)
                if mid:
                    normalise(m, 1)
                if front:
                    take_max(b, 0)
                if last:
                    add_experts(e, eu, 3)
                if mid:
                    oT_low(m)
                if front:
                    for i in range(1, 4):
                        take_max(b, i)
                if mid:
                    h_low(m, 0)
                if front:
                    take_max(b, 4)
                if last:
                    add_experts(e, eu, 4)
                if front:
                    take_max(b, 5)
                    stack_max(b)
                if mid:
                    h_low(m, 1)
                    add_mlp(m, mu)
                    second_norm_stats(m, mu)
                if last:
                    add_experts(e, eu, 5)
                if front:
                    qs_copy_b(b)
                if mid:
                    second_norm(m, mu)
                if last:
                    add_experts(e, eu, 6)
                if has(s, 1):
                    first_norm_stats(n_pair, n, nu)
                if mid:
                    x2T_low(m, mu)
                if has(s, 1):
                    first_norm(n, nu)
                if last:
                    add_experts(e, eu, 7)
                if mid:
                    gating(m, mu)

            first_norm_stats(0, 0, 0)
            first_norm(0, 0)
            run(dve, step)


_INS = ['x', 'ctx_768', 'g_xattn', 'g_ffn', 'L0_xattn_Wq', 'L0_xattn_bq', 'L0_xattn_Wk', 'L0_xattn_bk',
        'L0_xattn_Wv', 'L0_xattn_bv', 'L0_xattn_W1', 'L0_xattn_b1', 'L0_xattn_W2', 'L0_xattn_b2',
        'L0_ffn_gate_W', 'L0_ffn_gate_b', 'L0_ffn_expert_W', 'L0_ffn_expert_b']


def kernel(**inputs):
    import numpy as np
    import concourse.bacc as bacc
    from concourse.bass_utils import run_bass_kernel_spmd

    nc = bacc.Bacc("TRN2", target_bir_lowering=False, num_devices=1)
    arrays, args = {}, []
    for name in _INS:
        a = np.ascontiguousarray(inputs[name])
        arrays[f"in_{name}"] = a
        args.append(nc.dram_tensor(f"in_{name}", a.shape, mybir.dt.from_np(a.dtype), kind="ExternalInput").ap())
    args.append(nc.dram_tensor("out", (B, N, D), F32, kind="ExternalOutput").ap())
    gated_block(nc, *args)
    return run_bass_kernel_spmd(nc, [arrays], core_ids=[0]).results[0]["out"]
```

```python
from contextlib import ExitStack

import concourse.bass as bass
from concourse import mybir

F32 = mybir.dt.float32
F32R = mybir.dt.float32r
F16 = mybir.dt.float16
ALU = mybir.AluOpType
ACT = mybir.ActivationFunctionType
AX = mybir.AxisListType

P = 128
B, N, D = 32, 256, 256
M, DT = 77, 192
MP = M + M % 2
H = 16
DH = D // H
HID = 2 * D
E = 8
T = N // P
KC = D // P
HC = HID // P
YC = 96
YK = DT // YC
SLOT = 64
SHIFT = 3 * DH
PAIRS = H // 2
DV = DH + 1
LN_EPS = 1e-5
EPS, W_THRES, TOP_K = 1e-4, 0.1, 2
SCALE = float(DH) ** -0.5
MAX_CHUNKS = [[(0, 6)], [(6, 2), (8, 4)], [(12, 4)]]
CONSTS = 7 + E + 8
POOL_LOW = (1, 3, 5)
VECTOR_LOW = (0, 2, 4, 6, 7)
GATE_OPS = 22
STEADY = 4
LAST = B - 2


def gated_block(nc, x, y, g_xattn, g_ffn, Wq, bq, Wk, bk, Wv, bv, W1, b1, W2, b2,
                gate_W, gate_b, expert_W, expert_b, out):
    x_pairs = x.rearrange("(i u) (p t) d -> i u p t d", u=2, t=T)
    y_pairs = y.rearrange("(i u) m d -> i u m d", u=2)
    out_pairs = out.rearrange("(i u) (p t) d -> i u p t d", u=2, t=T)

    with ExitStack() as ctx:
        def sb(name, shape, dt=F32):
            return ctx.enter_context(nc.sbuf_tensor(name, shape, dt))

        def bank(name):
            return ctx.enter_context(nc.psum_tensor(name, [P, 512], F32))

        def sem(name):
            return ctx.enter_context(nc.semaphore(name))

        wq_f = sb("wq_f", [P, KC, D])
        w1_f = sb("w1_f", [P, KC, HID])
        w2_f = sb("w2_f", [P, HC, D])
        we_f = sb("we_f", [P, KC, E * D])
        gw_f = sb("gw_f", [P, KC, E])
        wq_hi, wq_lo = sb("wq_hi", [P, KC, D], F32R), sb("wq_lo", [P, KC, D], F32R)
        w1_hi, w1_lo = sb("w1_hi", [P, KC, HID], F32R), sb("w1_lo", [P, KC, HID], F32R)
        w2_hi, w2_lo = sb("w2_hi", [P, HC, D], F32R), sb("w2_lo", [P, HC, D], F32R)
        we_hi, we_lo = sb("we_hi", [P, KC, E * D], F32R), sb("we_lo", [P, KC, E * D], F32R)
        gw_hi, gw_lo = sb("gw_hi", [P, KC, E], F32R), sb("gw_lo", [P, KC, E], F32R)
        wkv = sb("wkv", [YC, YK, 2 * D])
        eb = sb("eb", [E, D])
        bq_rows = sb("bq_rows", [P, D])
        bkv_rows = sb("bkv_rows", [M, 2 * D])
        b2_rows = sb("b2_rows", [P, D])
        b2g_rows = sb("b2g_rows", [P, D])
        gb_rows = sb("gb_rows", [P, E])
        b1_cols = sb("b1_cols", [P, HC])
        gates = sb("gates", [P, 2])
        tanh_g = sb("tanh_g", [P, 2])
        ffn_scale = sb("ffn_scale", [P, 1])
        ident32 = sb("ident32", [P, P])
        ident16 = sb("ident16", [P, P], F16)
        own_head = sb("own_head", [P, PAIRS, M], F16)
        rank = sb("rank", [P, T, E])
        minus_half, ln_eps = sb("minus_half", [P, T]), sb("ln_eps", [P, T])

        x_sb = sb("x_sb", [P, 2, T, D])
        y_sb = sb("y_sb", [M, 2, DT])
        xb = sb("xb", [P, 2, T, D])
        stats1, mv1 = sb("stats1", [P, T, 6]), sb("mv1", [P, T, 2])
        ve1, rstd1 = sb("ve1", [P, T]), sb("rstd1", [P, T])
        xn = sb("xn", [P, T, D])
        xnT_hi, xnT_lo = sb("xnT_hi", [P, KC, N], F32R), sb("xnT_lo", [P, KC, N], F32R)
        yT = sb("yT", [YC, YK, M])
        kv = sb("kv", [M, 2 * D])
        q = sb("q", [P, T, D])
        v_hi, v_lo = sb("v_hi", [M, 2, H, DV], F16), sb("v_lo", [M, 2, H, DV], F16)
        k_hi, q_hi = sb("k_hi", [M, D], F16), sb("q_hi", [P, T, D], F16)
        k_stack = sb("k_stack", [M, H, SLOT], F16)
        q_stack = sb("q_stack", [P, T, H, SLOT], F16)
        qhT = sb("qhT", [P, KC, N], F16)
        khT = sb("khT", [P, KC, M], F16)
        k_block = sb("k_block", [P, H, M], F16)
        row_max = sb("row_max", [P, T, H])
        kz = sb("kz", [P, PAIRS, 2, M], F16)
        qsT = sb("qsT", [P, PAIRS, N], F16)
        RING = 4
        p_f = sb("p_f", [M, RING, 2 * N])
        p_hi = sb("p_hi", [M, RING, 2, N], F16)
        p_lo = sb("p_lo", [M, RING, 2, N], F16)
        rden = sb("rden", [P, 2, T, H // 2])
        o = sb("o", [P, T, D])
        oT_hi, oT_lo = sb("oT_hi", [P, KC, N], F32R), sb("oT_lo", [P, KC, N], F32R)
        h_f = sb("h_f", [P, HC, N])
        h_hi, h_lo = sb("h_hi", [P, HC, N], F32R), sb("h_lo", [P, HC, N], F32R)
        x1 = sb("x1", [P, 2, T, D])
        stats2, mv2 = sb("stats2", [P, T, 6]), sb("mv2", [P, T, 2])
        ve2, rstd2 = sb("ve2", [P, T]), sb("rstd2", [P, T])
        xn2 = sb("xn2", [P, T, D])
        x2T_hi, x2T_lo = sb("x2T_hi", [P, 2, KC, N], F32R), sb("x2T_lo", [P, 2, KC, N], F32R)
        gs, gshift, gexp, geq, gnot, gs2, gsel2, gmask, gp, gw = (
            sb(n, [P, T, E]) for n in ("gs", "gshift", "gexp", "geq", "gnot", "gs2", "gsel2", "gmask", "gp", "gw"))
        gm1, gf1, gm2, gf2, gsum, grs, gtot, grt = (
            sb(n, [P, T]) for n in ("gm1", "gf1", "gm2", "gf2", "gsum", "grs", "gtot", "grt"))
        comb = sb("comb", [P, 2, T, E])
        combT = sb("combT", [E, N])
        acc = sb("acc", [P, 2, T, D])

        G = [bank("g0"), bank("g1")]
        S = [bank("s0"), bank("s1")]
        TT = [bank("t0"), bank("t1")]
        X = [bank("e0"), bank("e1")]

        w_loaded = sem("w_loaded")
        consts_ready, waits_met = sem("consts_ready"), sem("waits_met")
        w_hi_ready, w_lo_ready = sem("w_hi_ready"), sem("w_lo_ready")
        tanh_ready, b2g_ready = sem("tanh_ready"), sem("b2g_ready")
        x_loaded = [sem("x_loaded0"), sem("x_loaded1")]
        y_loaded = [sem("y_loaded0"), sem("y_loaded1")]
        stats1_done, mv1_done = sem("stats1_done"), sem("mv1_done")
        ve1_done, rstd1_done, xn_done = sem("ve1_done"), sem("rstd1_done"), sem("xn_done")
        xb_done = sem("xb_done")
        xT_in_psum, yT_in_psum = sem("xT_in_psum"), sem("yT_in_psum")
        xnT_hi_done, xnT_lo_done, yT_done = sem("xnT_hi_done"), sem("xnT_lo_done"), sem("yT_done")
        kv_in_psum, q_in_psum = sem("kv_in_psum"), sem("q_in_psum")
        kv_done, q_done = sem("kv_done"), sem("q_done")
        v_split, k_split = sem("v_split"), sem("k_split")
        k_hi_done = sem("k_hi_done")
        q_hi_done, q_lo_done, q_stacked = sem("q_hi_done"), sem("q_lo_done"), sem("q_stacked")
        hiT_in_psum, qhT_done, khT_done = sem("hiT_in_psum"), sem("qhT_done"), sem("khT_done")
        k_block_done = sem("k_block_done")
        max_scores, max_taken = sem("max_scores"), sem("max_taken")
        max_hi_done, max_lo_done = sem("max_hi_done"), sem("max_lo_done")
        kz_in_psum, kz_done = sem("kz_in_psum"), sem("kz_done")
        qs_in_psum = sem("qs_in_psum")
        qsa_done, qsb_done = sem("qsa_done"), sem("qsb_done")
        scores_ready, exps_done = sem("scores_ready"), sem("exps_done")
        p_lo_vector, p_lo_pool = sem("p_lo_vector"), sem("p_lo_pool")
        av_done = sem("av_done")
        rden_done, o_done = sem("rden_done"), sem("o_done")
        oT_in_psum, oT_hi_done, oT_lo_done = sem("oT_in_psum"), sem("oT_hi_done"), sem("oT_lo_done")
        h_in_psum, relu_done = sem("h_in_psum"), sem("relu_done")
        h_lo_done = sem("h_lo_done")
        mlp_in_psum, x1_done = sem("mlp_in_psum"), sem("x1_done")
        stats2_done, mv2_done = sem("stats2_done"), sem("mv2_done")
        ve2_done, rstd2_done, xn2_done = sem("ve2_done"), sem("rstd2_done"), sem("xn2_done")
        x2T_in_psum, x2T_hi_done, x2T_lo_done = sem("x2T_in_psum"), sem("x2T_hi_done"), sem("x2T_lo_done")
        gate_in_psum, gate_op, gate_exp = sem("gate_in_psum"), sem("gate_op"), sem("gate_exp")
        combT_in_psum, combT_done = sem("combT_in_psum"), sem("combT_done")
        bias_in_psum, acc_started = sem("bias_in_psum"), sem("acc_started")
        expert_in_psum, expert_added = sem("expert_in_psum"), sem("expert_added")
        stored = [sem("stored0"), sem("stored1")]

        block = ctx.enter_context(nc.Block())
        WEIGHTS = 17

        def at_least(eng, semaphore, value):
            if not isinstance(value, int) or value > 0:
                eng.wait_ge(semaphore, value)

        def apart(eng):
            eng.sem_inc(waits_met, 1)

        def row(pair, u, d):
            return pair + (u + d) // 2, (u + d) % 2, 2 * pair + u + d

        def run(eng, step):
            for s in range(STEADY):
                step(s // 2, s % 2, s)
            with eng.Fori(STEADY // 2, LAST // 2) as pair:
                for u in range(2):
                    step(pair, u, STEADY + u)
            for s in range(LAST, B + 3):
                step(s // 2, s % 2, s)

        def rows_to(count):
            return min(count, B) if isinstance(count, int) else count

        def has(s, d):
            return 0 <= s + d < B

        @block.sync
        def _(sp):
            for dst, src in [(wq_f[:], Wq.rearrange("(k p) n -> p k n", p=P)),
                             (wkv[:, :, 0:D], Wk.rearrange("(k p) n -> p k n", p=YC)),
                             (wkv[:, :, D:2 * D], Wv.rearrange("(k p) n -> p k n", p=YC)),
                             (bq_rows[:], bq.partition_broadcast(P)),
                             (bkv_rows[:, 0:D], bk.partition_broadcast(M)),
                             (bkv_rows[:, D:2 * D], bv.partition_broadcast(M)),
                             (gates[:, 0:1], g_xattn.partition_broadcast(P)),
                             (gates[:, 1:2], g_ffn.partition_broadcast(P)),
                             (b2_rows[:], b2.partition_broadcast(P)),
                             (gb_rows[:], gate_b.partition_broadcast(P)),
                             (eb[:], expert_b[:]),
                             (w1_f[:], W1.rearrange("(k p) n -> p k n", p=P)),
                             (w2_f[:], W2.rearrange("(k p) n -> p k n", p=P)),
                             (gw_f[:], gate_W.rearrange("(k p) n -> p k n", p=P))]:
                sp.dma_start(dst, src).then_inc(w_loaded, 16)
            sp.dma_start(b1_cols[:], b1.rearrange("(c p) -> p c", p=P), allow_slow_non_contiguous=True).then_inc(w_loaded, 16)
            for k in range(KC):
                sp.dma_start(we_f[:, k, :].rearrange("p (e f) -> p e f", e=E),
                             expert_W[:, k * P:(k + 1) * P, :].rearrange("e p f -> p e f")).then_inc(w_loaded, 16)
            for u in range(2):
                sp.wait_ge(stored[u], 16 * (B // 2))

        @block.gpsimd
        def _(pool):
            pool.memset(ident32[:], 0.0).then_inc(consts_ready, 1)
            pool.memset(ident16[:], 0.0).then_inc(consts_ready, 1)
            pool.memset(own_head[:], 1.0).then_inc(consts_ready, 1)
            pool.wait_ge(consts_ready, 3)
            for m in (ident32, ident16):
                pool.affine_select(out=m[:], in_=m[:], compare_op=ALU.not_equal, fill=1.0, base=0,
                                   pattern=[[-1, P]], channel_multiplier=1).then_inc(consts_ready, 1)
            pool.affine_select(out=own_head[:], in_=own_head[:], compare_op=ALU.is_ge, fill=0.0, base=0,
                               pattern=[[-DH, PAIRS], [0, M]], channel_multiplier=1).then_inc(consts_ready, 1)
            pool.wait_ge(consts_ready, 6)
            pool.affine_select(out=own_head[:], in_=own_head[:], compare_op=ALU.is_ge, fill=0.0, base=DH - 1,
                               pattern=[[DH, PAIRS], [0, M]], channel_multiplier=-1).then_inc(consts_ready, 1)
            for e in range(E):
                pool.memset(rank[:, :, e:e + 1], float(E - e)).then_inc(consts_ready, 1)
            pool.memset(minus_half[:], -0.5).then_inc(consts_ready, 1)
            pool.memset(ln_eps[:], LN_EPS).then_inc(consts_ready, 1)
            pool.memset(k_stack[:, :, SHIFT:SHIFT + 2], -1.0).then_inc(consts_ready, 1)
            pool.memset(k_stack[:, :, SHIFT + 2:SLOT], 0.0).then_inc(consts_ready, 1)
            pool.memset(q_stack[:, :, :, SHIFT + 2:SLOT], 0.0).then_inc(consts_ready, 1)
            pool.memset(kz[:], 0.0).then_inc(consts_ready, 1)
            pool.memset(v_hi[:, :, :, DH:DV], 1.0).then_inc(consts_ready, 1)
            pool.memset(v_lo[:, :, :, DH:DV], 0.0).then_inc(consts_ready, 1)
            pool.wait_ge(consts_ready, CONSTS)

            def first_norm_scale(b):
                pool.wait_ge(mv1_done, 2 * b + 2)
                pool.tensor_tensor(ve1[:], mv1[:, :, 1], ln_eps[:], ALU.add).then_inc(ve1_done, 1)
                pool.wait_ge(ve1_done, b + 1)
                at_least(pool, xn_done, 2 * b)
                pool.tensor_tensor(rstd1[:], ve1[:], minus_half[:], ALU.pow).then_inc(rstd1_done, 1)

            def second_norm_scale(b):
                pool.wait_ge(mv2_done, 2 * b + 2)
                pool.tensor_tensor(ve2[:], mv2[:, :, 1], ln_eps[:], ALU.add).then_inc(ve2_done, 1)
                pool.wait_ge(ve2_done, b + 1)
                pool.tensor_tensor(rstd2[:], ve2[:], minus_half[:], ALU.pow).then_inc(rstd2_done, 1)

            def x_with_bias(b, u):
                at_least(pool, x1_done, b - 1)
                pool.tensor_tensor(xb[:, u], x_sb[:, u], b2g_rows[:].unsqueeze(1).to_broadcast([P, T, D]),
                                   ALU.add).then_inc(xb_done, 1)

            def p_low(b, g):
                r = g % RING
                pool.wait_ge(exps_done, 16 * b + 2 * g + 2)
                pool.tensor_tensor(p_lo[:, r].rearrange("m h n -> m (h n)"), p_f[:, r, :],
                                   p_hi[:, r].rearrange("m h n -> m (h n)"), ALU.subtract).then_inc(p_lo_pool, 1)

            def k_rest(b):
                pool.wait_ge(k_hi_done, b + 1)
                at_least(pool, kz_in_psum, b)
                high = k_hi[:].rearrange("m (h d) -> m h d", h=H)
                pool.tensor_tensor(k_stack[:, :, DH:2 * DH], kv[:, 0:D].rearrange("m (h d) -> m h d", h=H),
                                   high, ALU.subtract).then_inc(k_split, 1)
                pool.tensor_copy(k_stack[:, :, 0:DH], high).then_inc(k_split, 1)
                pool.tensor_copy(k_stack[:, :, 2 * DH:3 * DH], high).then_inc(k_split, 1)

            def q_low(b):
                pool.wait_ge(q_hi_done, b + 1)
                at_least(pool, qs_in_psum, 2 * b)
                pool.tensor_tensor(q_stack[:, :, :, 2 * DH:3 * DH].rearrange("p t h d -> p (t h) d"),
                                   q[:].rearrange("p t (h d) -> p (t h) d", h=H),
                                   q_hi[:].rearrange("p t (h d) -> p (t h) d", h=H),
                                   ALU.subtract).then_inc(q_lo_done, 1)

            def v_parts(b, u):
                at_least(pool, av_done, 8 * (b - 1))
                v = kv[:, D:2 * D].rearrange("m (h d) -> m h d", h=H)
                apart(pool)
                pool.tensor_copy(v_hi[:, u, :, 0:DH], v).then_inc(v_split, 1)
                pool.wait_ge(v_split, 2 * b + 1)
                pool.tensor_tensor(v_lo[:, u, :, 0:DH], v, v_hi[:, u, :, 0:DH], ALU.subtract).then_inc(v_split, 1)

            def key_blocks(b):
                pool.wait_ge(khT_done, b + 1)
                at_least(pool, max_scores, 6 * b)
                for c in range(KC):
                    pool.tensor_tensor(k_block[:, c * PAIRS:(c + 1) * PAIRS, :], own_head[:],
                                       khT[:, c, :].unsqueeze(1).to_broadcast([P, PAIRS, M]),
                                       ALU.mult).then_inc(k_block_done, 1)

            pool.wait_ge(b2g_ready, 1)
            pool.wait_ge(x_loaded[0], 16)
            first_norm_scale(0)
            x_with_bias(0, 0)

            def step(pair, u, s):
                _, _, b = row(pair, u, 0)
                _, mu, m = row(pair, u, -1)
                n_pair, nu, n = row(pair, u, 1)
                if has(s, -1):
                    for g in POOL_LOW:
                        p_low(m, g)
                if has(s, 0):
                    key_blocks(b)
                    k_rest(b)
                    q_low(b)
                    v_parts(b, u)
                if has(s, -1):
                    second_norm_scale(m)
                if has(s, 1):
                    first_norm_scale(n)
                    x_with_bias(n, nu)

            run(pool, step)

        @block.scalar
        def _(act):
            def load(pair, u, b):
                at_least(act, xn_done, 2 * (b - 1))
                at_least(act, xb_done, b - 1)
                act.dma_start(x_sb[:, u], x_pairs[pair, u]).then_inc(x_loaded[u], 16)
                at_least(act, yT_in_psum, b - 1)
                act.dma_start(y_sb[:, u], y_pairs[pair, u]).then_inc(y_loaded[u], 16)

            load(0, 0, 0)
            load(0, 1, 1)
            act.wait_ge(w_loaded, 16 * WEIGHTS)
            act.activation(tanh_g[:], gates[:], ACT.Tanh).then_inc(tanh_ready, 1)
            for hi, full in ((wq_hi, wq_f), (w1_hi, w1_f), (w2_hi, w2_f), (gw_hi, gw_f), (we_hi, we_f)):
                act.activation(hi[:], full[:], ACT.Copy).then_inc(w_hi_ready, 1)

            def xnT_high(b):
                act.wait_ge(xT_in_psum, b + 1)
                at_least(act, q_in_psum, b)
                act.activation(xnT_hi[:].rearrange("p k n -> p (k n)"), G[0][:], ACT.Copy).then_inc(xnT_hi_done, 1)

            def yT_copy(b):
                act.wait_ge(yT_in_psum, b + 1)
                at_least(act, kv_in_psum, b)
                act.activation(yT[:].rearrange("p k m -> p (k m)"), G[1][0:YC, 0:YK * M], ACT.Copy).then_inc(yT_done, 1)

            def combT_copy(b):
                act.wait_ge(combT_in_psum, b + 1)
                at_least(act, bias_in_psum, b)
                act.activation(combT[:], G[1][0:E, 0:N], ACT.Copy).then_inc(combT_done, 1)

            def exps(b, g):
                r = g % RING
                act.wait_ge(scores_ready, 8 * b + g + 1)
                at_least(act, av_done, 8 * b + g - RING + 1)
                act.activation(p_f[:, r, :], TT[g % 2][0:M, :], ACT.Exp, scale=SCALE).then_inc(exps_done, 1)
                act.activation(p_hi[:, r].rearrange("m h n -> m (h n)"), TT[g % 2][0:M, :], ACT.Exp,
                               scale=SCALE).then_inc(exps_done, 1)

            def k_high(b):
                act.wait_ge(kv_done, b + 1)
                at_least(act, hiT_in_psum, b)
                at_least(act, k_split, 3 * b)
                act.activation(k_hi[:], kv[:, 0:D], ACT.Copy).then_inc(k_hi_done, 1)

            def q_stack_high(b):
                act.wait_ge(q_hi_done, b + 1)
                at_least(act, qs_in_psum, 2 * b)
                act.activation(q_stack[:, :, :, 0:2 * DH].rearrange("p t h (c d) -> p (t h) c d", c=2),
                               q_hi[:].rearrange("p t (h d) -> p (t h) d", h=H).unsqueeze(2).to_broadcast([P, T * H, 2, DH]),
                               ACT.Copy).then_inc(q_stacked, 1)

            def highT_copies(b):
                act.wait_ge(hiT_in_psum, b + 1)
                at_least(act, k_block_done, 2 * b)
                at_least(act, max_scores, 6 * b)
                src = G[0][:].bitcast(F16)
                act.activation(khT[:], src[:, KC * N:KC * (N + MP)].rearrange("p (k m) -> p k m", k=KC)[:, :, 0:M],
                               ACT.Copy).then_inc(khT_done, 1)
                act.activation(qhT[:].rearrange("p k n -> p (k n)"), src[:, 0:KC * N], ACT.Copy).then_inc(qhT_done, 1)

            def oT_high(b):
                act.wait_ge(oT_in_psum, b + 1)
                at_least(act, h_in_psum, 2 * b)
                act.activation(oT_hi[:].rearrange("p k n -> p (k n)"), G[1][:], ACT.Copy).then_inc(oT_hi_done, 1)

            def relus(b, c):
                act.wait_ge(h_in_psum, 2 * b + c + 1)
                at_least(act, h_lo_done, 2 * b)
                at_least(act, mlp_in_psum, b)
                for j in range(2):
                    for to in (h_hi, h_f):
                        act.activation(to[:, 2 * c + j, :], G[c][:, j * N:(j + 1) * N], ACT.Relu,
                                       bias=b1_cols[:, 2 * c + j:2 * c + j + 1]).then_inc(relu_done, 1)

            def kz_copies(b):
                act.wait_ge(kz_in_psum, b + 1)
                at_least(act, scores_ready, 8 * b)
                src = G[0][:].bitcast(F16)[:, 0:PAIRS * MP].rearrange("p (j m) -> p j m", j=PAIRS)[:, :, 0:M]
                for e in range(2):
                    act.activation(kz[e * SLOT:(e + 1) * SLOT, :, e, :], src[e * SLOT:(e + 1) * SLOT],
                                   ACT.Copy).then_inc(kz_done, 1)

            def qs_copy_a(b):
                act.wait_ge(qs_in_psum, 2 * b + 1)
                act.activation(qsT[:, 0:4, :].rearrange("p j n -> p (j n)"), G[0][:].bitcast(F16), ACT.Copy).then_inc(qsa_done, 1)

            def x2T_high(b, u):
                act.wait_ge(x2T_in_psum, b + 1)
                at_least(act, expert_in_psum, 8 * (b - 1))
                at_least(act, gate_in_psum, b - 1)
                act.activation(x2T_hi[:, u].rearrange("p k n -> p (k n)"), G[0][:], ACT.Copy).then_inc(x2T_hi_done, 1)

            def gate_exps(b):
                act.wait_ge(gate_op, GATE_OPS * b + 4)
                act.activation(gexp[:], gshift[:], ACT.Exp).then_inc(gate_exp, 1)

            def store(pair, u, b):
                act.wait_ge(expert_added, 16 * b + 16)
                act.dma_start(out_pairs[pair, u], acc[:, u]).then_inc(stored[u], 16)

            def step(pair, u, s):
                _, _, b = row(pair, u, 0)
                _, mu, m = row(pair, u, -1)
                _, _, e = row(pair, u, -2)
                f_pair, fu, f = row(pair, u, -3)
                l_pair, lu, l = row(pair, u, 2)
                front, mid = has(s, 0), has(s, -1)
                if front:
                    xnT_high(b)
                if mid:
                    exps(m, 0)
                    exps(m, 1)
                if front:
                    yT_copy(b)
                if has(s, -2):
                    gate_exps(e)
                if mid:
                    exps(m, 2)
                    exps(m, 3)
                if front:
                    k_high(b)
                if mid:
                    exps(m, 4)
                    exps(m, 5)
                    exps(m, 6)
                if front:
                    highT_copies(b)
                    q_stack_high(b)
                if mid:
                    exps(m, 7)
                if has(s, -3):
                    store(f_pair, fu, f)
                if has(s, -2):
                    combT_copy(e)
                if mid:
                    oT_high(m)
                    relus(m, 0)
                    relus(m, 1)
                if front:
                    kz_copies(b)
                    qs_copy_a(b)
                if has(s, 2):
                    load(l_pair, lu, l)
                if mid:
                    x2T_high(m, mu)

            run(act, step)

        @block.tensor
        def _(pe):
            pe.wait_ge(consts_ready, CONSTS)
            pe.wait_ge(w_loaded, 16 * WEIGHTS)
            pe.wait_ge(w_hi_ready, 5)
            pe.wait_ge(w_lo_ready, 5)

            def split_product(out_ap, pairs):
                n = 3 * len(pairs)
                i = 0
                for s_hi, s_lo, m_hi, m_lo in pairs:
                    for a, c in ((s_lo, m_hi), (s_hi, m_lo), (s_hi, m_hi)):
                        mm = pe.matmul(out_ap, a, c, start=(i == 0), stop=(i == n - 1))
                        i += 1
                return mm

            def transposes_xy(b, u):
                pe.wait_ge(xn_done, 2 * b + 2)
                at_least(pe, x2T_lo_done, b - 1)
                at_least(pe, qsa_done, b)
                for k in range(KC):
                    for t in range(T):
                        mm = pe.transpose(G[0][:, k * N + t * P:k * N + (t + 1) * P], xn[:, t, k * P:(k + 1) * P], ident32[:])
                mm.then_inc(xT_in_psum, 1)

            def transposes_y(pair, b, u):
                pe.wait_ge(y_loaded[u], 16 * (pair + 1))
                at_least(pe, gate_op, GATE_OPS * (b - 2) + 1)
                at_least(pe, qsb_done, b)
                for k in range(YK):
                    mm = pe.transpose(G[1][0:YC, k * M:(k + 1) * M], y_sb[:, u, k * YC:(k + 1) * YC], ident32[0:M, 0:M])
                mm.then_inc(yT_in_psum, 1)

            def scores(b, g):
                if g == 0:
                    pe.wait_ge(kz_done, 2 * b + 2)
                    pe.wait_ge(qsa_done, b + 1)
                    pe.wait_ge(qsb_done, b + 1)
                at_least(pe, exps_done, 2 * (8 * b + g - 1))
                for e in range(2):
                    mm = pe.matmul(TT[g % 2][0:M, e * N:(e + 1) * N], kz[:, g, e, :], qsT[:, g, :],
                                   start=True, stop=True)
                mm.then_inc(scores_ready, 1)

            def attend(b, u, g):
                if g == 0:
                    pe.wait_ge(v_split, 2 * b + 2)
                    pe.wait_ge(max_taken, 6 * b + 6)
                if g in VECTOR_LOW:
                    pe.wait_ge(p_lo_vector, len(VECTOR_LOW) * b + VECTOR_LOW.index(g) + 1)
                else:
                    pe.wait_ge(p_lo_pool, len(POOL_LOW) * b + POOL_LOW.index(g) + 1)
                r, half = g % RING, g // 4
                for e in range(2):
                    h = 2 * g + e
                    for t in range(T):
                        at = (t * (H // 2) + h % (H // 2)) * DV
                        hi, lo = p_hi[:, r, e, t * P:(t + 1) * P], p_lo[:, r, e, t * P:(t + 1) * P]
                        dst = S[half][:, at:at + DV]
                        pe.matmul(dst, lo, v_hi[:, u, h, :], start=True, stop=False)
                        pe.matmul(dst, hi, v_lo[:, u, h, :], start=False, stop=False)
                        mm = pe.matmul(dst, hi, v_hi[:, u, h, :], start=False, stop=True)
                mm.then_inc(av_done, 1)

            def combT_transposes(b, u):
                pe.wait_ge(gate_op, GATE_OPS * b + GATE_OPS)
                at_least(pe, q_done, rows_to(b + 3))
                for t in range(T):
                    mm = pe.transpose(G[1][0:E, t * P:(t + 1) * P], comb[:, u, t, :], ident32[:])
                mm.then_inc(combT_in_psum, 1)

            def expert_biases(b):
                pe.wait_ge(combT_done, b + 1)
                pe.wait_ge(x2T_lo_done, b + 1)
                at_least(pe, qhT_done, rows_to(b + 3))
                for t in range(T):
                    mm = pe.matmul(G[0][:, t * D:(t + 1) * D], combT[:, t * P:(t + 1) * P], eb[:], start=True, stop=True)
                mm.then_inc(bias_in_psum, 1)

            def keys_values(b):
                pe.wait_ge(yT_done, b + 1)
                pe.wait_ge(xnT_lo_done, b + 1)
                for k in range(YK):
                    mm = pe.matmul(G[0][0:M, :], yT[:, k, :], wkv[:, k, :], start=(k == 0), stop=(k == YK - 1))
                mm.then_inc(kv_in_psum, 1)

            def queries(b):
                pe.wait_ge(xnT_lo_done, b + 1)
                pe.wait_ge(yT_done, b + 1)
                for t in range(T):
                    rows = slice(t * P, (t + 1) * P)
                    mm = split_product(G[1][:, t * D:(t + 1) * D],
                                       [(xnT_hi[:, k, rows], xnT_lo[:, k, rows], wq_hi[:, k, :], wq_lo[:, k, :])
                                        for k in range(KC)])
                mm.then_inc(q_in_psum, 1)

            def high_transposes(b):
                pe.wait_ge(q_hi_done, b + 1)
                pe.wait_ge(k_hi_done, b + 1)
                pe.wait_ge(kv_done, b + 1)
                dst = G[0][:].bitcast(F16)
                for c in range(KC):
                    for t in range(T):
                        pe.transpose(dst[:, c * N + t * P:c * N + (t + 1) * P], q_hi[:, t, c * P:(c + 1) * P], ident16[:])
                    mm = pe.transpose(dst[:, KC * N + c * MP:KC * N + c * MP + M], k_hi[:, c * P:(c + 1) * P],
                                      ident16[0:M, 0:M])
                mm.then_inc(hiT_in_psum, 1)

            def scores_for_max(b, i):
                t, c = divmod(i, len(MAX_CHUNKS))
                if i == 0:
                    pe.wait_ge(qhT_done, b + 1)
                    pe.wait_ge(k_block_done, 2 * b + 2)
                if i < 2:
                    at_least(pe, o_done, 4 * b - 2 + 2 * i)
                else:
                    pe.wait_ge(max_taken, 6 * b + i - 1)
                at = 0
                for h, n in MAX_CHUNKS[c]:
                    mm = pe.matmul(S[i % 2][:, at * M:(at + n) * M], qhT[:, h // PAIRS, t * P:(t + 1) * P],
                                   k_block[:, h:h + n, :], start=True, stop=True)
                    at += n
                mm.then_inc(max_scores, 1)

            def output_transposes(b):
                pe.wait_ge(o_done, 4 * b + 4)
                at_least(pe, q_done, rows_to(b + 2))
                at_least(pe, combT_done, b)
                for k in range(KC):
                    for t in range(T):
                        mm = pe.transpose(G[1][:, k * N + t * P:k * N + (t + 1) * P], o[:, t, k * P:(k + 1) * P], ident32[:])
                mm.then_inc(oT_in_psum, 1)

            def mlp_up(b, c):
                pe.wait_ge(oT_lo_done, b + 1)
                if c == 0:
                    at_least(pe, acc_started, b)
                    at_least(pe, qhT_done, rows_to(b + 2))
                for j in range(2):
                    cols = slice((2 * c + j) * P, (2 * c + j + 1) * P)
                    mm = split_product(G[c][:, j * N:(j + 1) * N],
                                       [(w1_hi[:, k, cols], w1_lo[:, k, cols], oT_hi[:, k, :], oT_lo[:, k, :])
                                        for k in range(KC)])
                mm.then_inc(h_in_psum, 1)

            def mlp_down(b):
                pe.wait_ge(h_lo_done, 2 * b + 2)
                pe.wait_ge(relu_done, 8 * b + 8)
                for t in range(T):
                    rows = slice(t * P, (t + 1) * P)
                    mm = split_product(G[1][:, t * D:(t + 1) * D],
                                       [(h_hi[:, c, rows], h_lo[:, c, rows], w2_hi[:, c, :], w2_lo[:, c, :])
                                        for c in range(HC)])
                mm.then_inc(mlp_in_psum, 1)

            def key_stack_transposes(b):
                pe.wait_ge(k_split, 3 * b + 3)
                at_least(pe, relu_done, 8 * (b - 1) + 4)
                pe.wait_ge(qhT_done, b + 1)
                dst = G[0][:].bitcast(F16)
                for j in range(PAIRS):
                    mm = pe.transpose(dst[:, j * MP:j * MP + M], k_stack[:, 2 * j:2 * j + 2, :].rearrange("m h r -> m (h r)"),
                                      ident16[0:M, 0:M])
                mm.then_inc(kz_in_psum, 1)

            def query_stack_transposes(b, c):
                if c == 0:
                    pe.wait_ge(q_lo_done, b + 1)
                    pe.wait_ge(q_stacked, b + 1)
                    pe.wait_ge(max_lo_done, b + 1)
                    pe.wait_ge(kz_done, 2 * b + 2)
                else:
                    at_least(pe, x1_done, b)
                    pe.wait_ge(q_done, b + 1)
                dst = G[c][:].bitcast(F16)
                for j in range(4):
                    for t in range(T):
                        mm = pe.transpose(dst[:, j * N + t * P:j * N + (t + 1) * P],
                                          q_stack[:, t, 8 * c + 2 * j:8 * c + 2 * j + 2, :].rearrange("p h r -> p (h r)"),
                                          ident16[:])
                mm.then_inc(qs_in_psum, 1)

            def second_norm_transposes(b):
                pe.wait_ge(xn2_done, 2 * b + 2)
                at_least(pe, qsa_done, rows_to(b + 2))
                for k in range(KC):
                    for t in range(T):
                        mm = pe.transpose(G[0][:, k * N + t * P:k * N + (t + 1) * P], xn2[:, t, k * P:(k + 1) * P], ident32[:])
                mm.then_inc(x2T_in_psum, 1)

            def gate_scores(b, u):
                pe.wait_ge(x2T_lo_done, b + 1)
                at_least(pe, qsb_done, rows_to(b + 2))
                for t in range(T):
                    rows = slice(t * P, (t + 1) * P)
                    mm = split_product(G[1][:, t * E:(t + 1) * E],
                                       [(x2T_hi[:, u, k, rows], x2T_lo[:, u, k, rows], gw_hi[:, k, :], gw_lo[:, k, :])
                                        for k in range(KC)])
                mm.then_inc(gate_in_psum, 1)

            def experts(b, u, i):
                t, c = i % T, i // T
                at_least(pe, expert_added, 16 * b + 2 * (i - 1))
                rows, cols = slice(t * P, (t + 1) * P), slice(c * 2 * D, (c + 1) * 2 * D)
                mm = split_product(X[i % 2][:],
                                   [(x2T_hi[:, u, k, rows], x2T_lo[:, u, k, rows], we_hi[:, k, cols], we_lo[:, k, cols])
                                    for k in range(KC)])
                mm.then_inc(expert_in_psum, 1)

            def step(pair, u, s):
                _, _, b = row(pair, u, 0)
                _, mu, m = row(pair, u, -1)
                _, eu, e = row(pair, u, -2)
                _, fu, f = row(pair, u, -3)
                front, mid, first, last = has(s, 0), has(s, -1), has(s, -2), has(s, -3)
                if front:
                    transposes_xy(b, u)
                if mid:
                    scores(m, 0)
                    scores(m, 1)
                if last:
                    experts(f, fu, 4)
                if front:
                    transposes_y(pair, b, u)
                if mid:
                    attend(m, mu, 0)
                    scores(m, 2)
                if last:
                    experts(f, fu, 5)
                if front:
                    keys_values(b)
                if mid:
                    attend(m, mu, 1)
                    scores(m, 3)
                    attend(m, mu, 2)
                    scores(m, 4)
                if front:
                    queries(b)
                if last:
                    experts(f, fu, 6)
                if mid:
                    attend(m, mu, 3)
                    scores(m, 5)
                    attend(m, mu, 4)
                    scores(m, 6)
                if front:
                    high_transposes(b)
                if last:
                    experts(f, fu, 7)
                if mid:
                    attend(m, mu, 5)
                    scores(m, 7)
                    attend(m, mu, 6)
                    attend(m, mu, 7)
                if first:
                    combT_transposes(e, eu)
                if front:
                    scores_for_max(b, 0)
                if first:
                    expert_biases(e)
                if front:
                    scores_for_max(b, 1)
                if mid:
                    output_transposes(m)
                if first:
                    experts(e, eu, 0)
                if front:
                    scores_for_max(b, 2)
                if mid:
                    mlp_up(m, 0)
                if front:
                    scores_for_max(b, 3)
                if mid:
                    mlp_up(m, 1)
                if front:
                    scores_for_max(b, 4)
                if first:
                    experts(e, eu, 1)
                if front:
                    scores_for_max(b, 5)
                    key_stack_transposes(b)
                if mid:
                    mlp_down(m)
                if first:
                    experts(e, eu, 2)
                if front:
                    query_stack_transposes(b, 0)
                    query_stack_transposes(b, 1)
                if mid:
                    second_norm_transposes(m)
                if first:
                    experts(e, eu, 3)
                if mid:
                    gate_scores(m, mu)

            run(pe, step)

        @block.vector
        def _(dve):
            for i, (lo, hi, full) in enumerate(((wq_lo, wq_hi, wq_f), (w1_lo, w1_hi, w1_f), (w2_lo, w2_hi, w2_f),
                                                (gw_lo, gw_hi, gw_f), (we_lo, we_hi, we_f))):
                dve.wait_ge(w_hi_ready, i + 1)
                if i == 0:
                    dve.wait_ge(w_loaded, 16 * WEIGHTS)
                dve.tensor_tensor(lo[:], full[:], hi[:].bitcast(F32), ALU.subtract).then_inc(w_lo_ready, 1)
            dve.wait_ge(tanh_ready, 1)
            dve.tensor_scalar(b2g_rows[:], b2_rows[:], tanh_g[:, 0:1], None, ALU.mult).then_inc(b2g_ready, 1)
            dve.tensor_scalar(ffn_scale[:], tanh_g[:, 1:2], 1.0 / TOP_K, None, ALU.mult).then_inc(b2g_ready, 1)
            dve.wait_ge(b2g_ready, 2)
            dve.wait_ge(consts_ready, CONSTS)

            def first_norm_stats(pair, b, u):
                dve.wait_ge(x_loaded[u], 16 * (pair + 1))
                for t in range(T):
                    dve.bn_stats(stats1[:, t, :], x_sb[:, u, t, :]).then_inc(stats1_done, 1)
                for t in range(T):
                    dve.wait_ge(stats1_done, 2 * b + t + 1)
                    apart(dve)
                    dve.bn_aggr(mv1[:, t, :], stats1[:, t, :]).then_inc(mv1_done, 1)

            def first_norm(b, u):
                dve.wait_ge(rstd1_done, b + 1)
                dve.wait_ge(mv1_done, 2 * b + 2)
                at_least(dve, xT_in_psum, b)
                for t in range(T):
                    dve.tensor_scalar(xn[:, t, :], x_sb[:, u, t, :], mv1[:, t, 0:1], rstd1[:, t:t + 1],
                                      ALU.subtract, ALU.mult).then_inc(xn_done, 1)

            def xnT_low(b):
                dve.wait_ge(xnT_hi_done, b + 1)
                dve.tensor_tensor(xnT_lo[:].rearrange("p k n -> p (k n)"), G[0][:],
                                  xnT_hi[:].bitcast(F32).rearrange("p k n -> p (k n)"), ALU.subtract).then_inc(xnT_lo_done, 1)

            def p_low(b, g):
                r = g % RING
                dve.wait_ge(exps_done, 16 * b + 2 * g + 2)
                dve.tensor_tensor(p_lo[:, r].rearrange("m h n -> m (h n)"), p_f[:, r, :],
                                  p_hi[:, r].rearrange("m h n -> m (h n)"), ALU.subtract).then_inc(p_lo_vector, 1)

            def start_acc(pair, b, u):
                dve.wait_ge(bias_in_psum, b + 1)
                at_least(dve, stored[u], 16 * pair)
                dve.tensor_tensor(acc[:, u].rearrange("p t d -> p (t d)"), G[0][:],
                                  x1[:, u].rearrange("p t d -> p (t d)"), ALU.add).then_inc(acc_started, 1)

            def add_experts(b, u, i):
                t, c = i % T, i // T
                dve.wait_ge(expert_in_psum, 8 * b + i + 1)
                if i < 2:
                    dve.wait_ge(acc_started, b + 1)
                for j in range(2):
                    if j == 1:
                        dve.wait_ge(expert_added, 16 * b + 2 * i + 1)
                    elif i >= 2:
                        dve.wait_ge(expert_added, 16 * b + 2 * i - 2)
                    dve.scalar_tensor_tensor(out=acc[:, u, t, :], in0=X[i % 2][:, j * D:(j + 1) * D],
                                             scalar=comb[:, u, t, 2 * c + j:2 * c + j + 1], in1=acc[:, u, t, :],
                                             op0=ALU.mult, op1=ALU.add).then_inc(expert_added, 1)

            def kv_with_bias(b):
                dve.wait_ge(kv_in_psum, b + 1)
                at_least(dve, k_split, 3 * b)
                at_least(dve, v_split, 2 * b)
                dve.tensor_tensor(kv[:], G[0][0:M, :], bkv_rows[:], ALU.add).then_inc(kv_done, 1)

            def q_with_bias(b):
                dve.wait_ge(q_in_psum, b + 1)
                at_least(dve, q_lo_done, b)
                dve.tensor_tensor(q[:], G[1][:].rearrange("p (t d) -> p t d", t=T),
                                  bq_rows[:].unsqueeze(1).to_broadcast([P, T, D]), ALU.add).then_inc(q_done, 1)
                dve.wait_ge(q_done, b + 1)
                at_least(dve, hiT_in_psum, b)
                at_least(dve, q_stacked, b)
                dve.tensor_copy(q_hi[:], q[:]).then_inc(q_hi_done, 1)

            def normalise(b, half):
                dve.wait_ge(av_done, 8 * b + 4 * half + 4)
                src = S[half][:, 0:T * (H // 2) * DV].rearrange("p (t h d) -> p t h d", t=T, h=H // 2)
                dve.reciprocal(rden[:, half], src[:, :, :, DH]).then_inc(rden_done, 1)
                dve.wait_ge(rden_done, 2 * b + half + 1)
                if half == 0:
                    at_least(dve, oT_in_psum, b)
                for t in range(T):
                    dve.tensor_tensor(o[:, t, half * P:(half + 1) * P].rearrange("p (h d) -> p h d", h=H // 2),
                                      src[:, t, :, 0:DH],
                                      rden[:, half, t, :].unsqueeze(2).to_broadcast([P, H // 2, DH]),
                                      ALU.mult).then_inc(o_done, 1)

            def take_max(b, i):
                t, c = divmod(i, len(MAX_CHUNKS))
                h, n = MAX_CHUNKS[c][0][0], sum(k for _, k in MAX_CHUNKS[c])
                dve.wait_ge(max_scores, 6 * b + i + 1)
                if i == 0:
                    at_least(dve, max_lo_done, b)
                dve.tensor_reduce(row_max[:, t, h:h + n], S[i % 2][:, 0:n * M].rearrange("p (h m) -> p h m", h=n),
                                  AX.X, ALU.max).then_inc(max_taken, 1)

            def stack_max(b):
                dve.wait_ge(max_taken, 6 * b + 6)
                at_least(dve, qs_in_psum, 2 * b)
                flat = q_stack[:].rearrange("p t h r -> p (t h) r")
                mx = row_max[:].rearrange("p t h -> p (t h)")
                dve.tensor_copy(flat[:, :, SHIFT], mx).then_inc(max_hi_done, 1)
                dve.wait_ge(max_hi_done, b + 1)
                dve.tensor_tensor(flat[:, :, SHIFT + 1], mx, flat[:, :, SHIFT], ALU.subtract).then_inc(max_lo_done, 1)

            def oT_low(b):
                dve.wait_ge(oT_hi_done, b + 1)
                dve.tensor_tensor(oT_lo[:].rearrange("p k n -> p (k n)"), G[1][:],
                                  oT_hi[:].bitcast(F32).rearrange("p k n -> p (k n)"), ALU.subtract).then_inc(oT_lo_done, 1)

            def h_low(b, c):
                dve.wait_ge(relu_done, 8 * b + 4 * c + 4)
                part = slice(2 * c, 2 * c + 2)
                dve.tensor_tensor(h_lo[:, part, :], h_f[:, part, :], h_hi[:, part, :].bitcast(F32),
                                  ALU.subtract).then_inc(h_lo_done, 1)

            def add_mlp(b, u):
                dve.wait_ge(mlp_in_psum, b + 1)
                dve.wait_ge(xb_done, b + 1)
                dve.scalar_tensor_tensor(out=x1[:, u].rearrange("p t d -> p (t d)"), in0=G[1][:], scalar=tanh_g[:, 0:1],
                                         in1=xb[:, u].rearrange("p t d -> p (t d)"), op0=ALU.mult, op1=ALU.add)\
                   .then_inc(x1_done, 1)

            def second_norm_stats(b, u):
                dve.wait_ge(x1_done, b + 1)
                for t in range(T):
                    dve.bn_stats(stats2[:, t, :], x1[:, u, t, :]).then_inc(stats2_done, 1)
                for t in range(T):
                    dve.wait_ge(stats2_done, 2 * b + t + 1)
                    apart(dve)
                    dve.bn_aggr(mv2[:, t, :], stats2[:, t, :]).then_inc(mv2_done, 1)

            def second_norm(b, u):
                dve.wait_ge(rstd2_done, b + 1)
                for t in range(T):
                    dve.tensor_scalar(xn2[:, t, :], x1[:, u, t, :], mv2[:, t, 0:1], rstd2[:, t:t + 1],
                                      ALU.subtract, ALU.mult).then_inc(xn2_done, 1)

            def x2T_low(b, u):
                dve.wait_ge(x2T_hi_done, b + 1)
                dve.tensor_tensor(x2T_lo[:, u].rearrange("p k n -> p (k n)"), G[0][:],
                                  x2T_hi[:, u].bitcast(F32).rearrange("p k n -> p (k n)"), ALU.subtract).then_inc(x2T_lo_done, 1)

            def qs_copy_b(b):
                dve.wait_ge(qs_in_psum, 2 * b + 2)
                dve.tensor_copy(qsT[:, 4:8, :].rearrange("p j n -> p (j n)"), G[1][:].bitcast(F16)).then_inc(qsb_done, 1)

            def link(b, k, ins):
                ins.then_inc(gate_op, 1)
                dve.wait_ge(gate_op, GATE_OPS * b + k)

            def wide(a):
                return a[:].unsqueeze(2).to_broadcast([P, T, E])

            def gate_logits(b):
                dve.wait_ge(gate_in_psum, b + 1)
                link(b, 1, dve.tensor_tensor(gs[:], G[1][:, 0:T * E].rearrange("p (t e) -> p t e", t=T),
                                             gb_rows[:].unsqueeze(1).to_broadcast([P, T, E]), ALU.add))
                link(b, 2, dve.tensor_scalar(gs[:], gs[:], EPS, None, ALU.max))
                link(b, 3, dve.tensor_reduce(gm1[:], gs[:], AX.X, ALU.max))
                link(b, 4, dve.tensor_tensor(gshift[:], gs[:], wide(gm1), ALU.subtract))

            def gate_best(b):
                link(b, 5, dve.tensor_tensor(geq[:], gs[:], wide(gm1), ALU.is_equal))
                link(b, 6, dve.tensor_tensor(geq[:], geq[:], rank[:], ALU.mult))
                link(b, 7, dve.tensor_reduce(gf1[:], geq[:], AX.X, ALU.max))
                link(b, 8, dve.tensor_tensor(gnot[:], rank[:], wide(gf1), ALU.not_equal))
                link(b, 9, dve.tensor_tensor(gs2[:], gs[:], gnot[:], ALU.mult))
                link(b, 10, dve.tensor_reduce(gm2[:], gs2[:], AX.X, ALU.max))

            def gate_second(b):
                link(b, 11, dve.tensor_tensor(geq[:], gs2[:], wide(gm2), ALU.is_equal))
                link(b, 12, dve.tensor_tensor(geq[:], geq[:], rank[:], ALU.mult))
                link(b, 13, dve.tensor_reduce(gf2[:], geq[:], AX.X, ALU.max))
                link(b, 14, dve.tensor_tensor(gsel2[:], rank[:], wide(gf2), ALU.is_equal))
                link(b, 15, dve.scalar_tensor_tensor(out=gmask[:], in0=gsel2[:], scalar=1.0, in1=gnot[:],
                                                     op0=ALU.add, op1=ALU.subtract))

            def gate_weights(b, u):
                dve.wait_ge(gate_exp, b + 1)
                link(b, 16, dve.tensor_reduce(gsum[:], gexp[:], AX.X, ALU.add))
                link(b, 17, dve.reciprocal(grs[:], gsum[:]))
                link(b, 18, dve.tensor_tensor(gp[:], gexp[:], wide(grs), ALU.mult))
                link(b, 19, dve.scalar_tensor_tensor(out=gw[:], in0=gp[:], scalar=W_THRES, in1=gmask[:],
                                                     op0=ALU.max, op1=ALU.mult))
                link(b, 20, dve.tensor_reduce(gtot[:], gw[:], AX.X, ALU.add))
                link(b, 21, dve.reciprocal(grt[:], gtot[:]))
                link(b, 22, dve.scalar_tensor_tensor(out=comb[:, u], in0=gw[:], scalar=ffn_scale[:, 0:1], in1=wide(grt),
                                                     op0=ALU.mult, op1=ALU.mult))

            def step(pair, u, s):
                _, _, b = row(pair, u, 0)
                _, mu, m = row(pair, u, -1)
                e_pair, eu, e = row(pair, u, -2)
                _, fu, f = row(pair, u, -3)
                n_pair, nu, n = row(pair, u, 1)
                front, mid, first, last = has(s, 0), has(s, -1), has(s, -2), has(s, -3)
                if first:
                    gate_logits(e)
                if front:
                    xnT_low(b)
                if mid:
                    p_low(m, 0)
                if first:
                    gate_best(e)
                if mid:
                    p_low(m, 2)
                if last:
                    add_experts(f, fu, 4)
                if front:
                    kv_with_bias(b)
                if first:
                    gate_second(e)
                if last:
                    add_experts(f, fu, 5)
                if mid:
                    p_low(m, 4)
                if front:
                    q_with_bias(b)
                if first:
                    gate_weights(e, eu)
                if mid:
                    normalise(m, 0)
                    p_low(m, 6)
                if last:
                    add_experts(f, fu, 6)
                if mid:
                    p_low(m, 7)
                if last:
                    add_experts(f, fu, 7)
                if mid:
                    normalise(m, 1)
                if front:
                    take_max(b, 0)
                if first:
                    start_acc(e_pair, e, eu)
                if front:
                    take_max(b, 1)
                if mid:
                    oT_low(m)
                if first:
                    add_experts(e, eu, 0)
                if front:
                    take_max(b, 2)
                    take_max(b, 3)
                if mid:
                    h_low(m, 0)
                if front:
                    take_max(b, 4)
                if mid:
                    h_low(m, 1)
                if first:
                    add_experts(e, eu, 1)
                if front:
                    take_max(b, 5)
                    stack_max(b)
                if mid:
                    add_mlp(m, mu)
                    second_norm_stats(m, mu)
                if first:
                    add_experts(e, eu, 2)
                if front:
                    qs_copy_b(b)
                if mid:
                    second_norm(m, mu)
                if has(s, 1):
                    first_norm_stats(n_pair, n, nu)
                if mid:
                    x2T_low(m, mu)
                if has(s, 1):
                    first_norm(n, nu)
                if first:
                    add_experts(e, eu, 3)

            first_norm_stats(0, 0, 0)
            first_norm(0, 0)
            run(dve, step)


_INS = ['x', 'ctx_768', 'g_xattn', 'g_ffn', 'L0_xattn_Wq', 'L0_xattn_bq', 'L0_xattn_Wk', 'L0_xattn_bk',
        'L0_xattn_Wv', 'L0_xattn_bv', 'L0_xattn_W1', 'L0_xattn_b1', 'L0_xattn_W2', 'L0_xattn_b2',
        'L0_ffn_gate_W', 'L0_ffn_gate_b', 'L0_ffn_expert_W', 'L0_ffn_expert_b']


def kernel(**inputs):
    import numpy as np
    import concourse.bacc as bacc
    from concourse.bass_utils import run_bass_kernel_spmd

    nc = bacc.Bacc("TRN2", target_bir_lowering=False, num_devices=1)
    arrays, args = {}, []
    for name in _INS:
        a = np.ascontiguousarray(inputs[name])
        arrays[f"in_{name}"] = a
        args.append(nc.dram_tensor(f"in_{name}", a.shape, mybir.dt.from_np(a.dtype), kind="ExternalInput").ap())
    args.append(nc.dram_tensor("out", (B, N, D), F32, kind="ExternalOutput").ap())
    gated_block(nc, *args)
    return run_bass_kernel_spmd(nc, [arrays], core_ids=[0]).results[0]["out"]
```
